# Optimizing a Trainium2 kernel written in Bass

```python
import numpy as np
import jax
import jax.numpy as jnp

def _softmax(x, axis=-1):
    return jax.nn.softmax(x, axis=axis)

def _gelu(x):
    return jax.nn.gelu(x, approximate=True)

def _silu(x):
    return jax.nn.silu(x)

def _sigmoid(x):
    return jax.nn.sigmoid(x)

def _layernorm(x, axis=-1, eps=1e-05):
    m = jnp.mean(x, axis=axis, keepdims=True)
    v = jnp.var(x, axis=axis, keepdims=True)
    return (x - m) / jnp.sqrt(v + eps)

def _scatter_add(tgt, idx, src, axis=0):
    return tgt.at[idx].add(src)

def _segment_sum(src, seg, n):
    return jax.ops.segment_sum(src, seg, n)
kernel_name = 'mk_decoder_postln_d1_seqx_r8_1b6bd1'

def setup_inputs(seed: int=0):
    np.random.seed(seed)
    _w = jnp.asarray

    def _rec_inputs():
        import jax
        import jax.numpy as jnp
        _rk = jax.random.key(seed)
        x = -0.0003929 + 0.9999 * jax.random.normal(jax.random.fold_in(_rk, 1), (4, 256, 256), jnp.float32)
        _lenS = 256 - jax.random.randint(jax.random.fold_in(_rk, 7), (4,), 0, max(1, 256 // 4) + 1, jnp.int32)
        _lenS2 = 1601 - jax.random.randint(jax.random.fold_in(_rk, 8), (4,), 0, max(1, 1601 // 4) + 1, jnp.int32)
        _ctx_2048P = jax.random.normal(jax.random.fold_in(_rk, 11), (4, 16, 256), jnp.float32)
        _ctx_2048c = jax.random.dirichlet(jax.random.fold_in(_rk, 511), 0.3 * jnp.ones((16,), jnp.float32), (4, 1601))
        _ctx_2048t = jnp.einsum('bsk,bkd->bsd', _ctx_2048c, _ctx_2048P)
        _ctx_2048t = _ctx_2048t * jax.lax.rsqrt(jnp.mean(jnp.square(_ctx_2048t)) + 1e-12) * 0.953939
        ctx_2048 = -0.000514642 + 1.00011 * (_ctx_2048t + 0.3 * jax.random.normal(jax.random.fold_in(_rk, 611), (4, 1601, 256), jnp.float32))
        return (x, ctx_2048)
    x, ctx_2048 = _rec_inputs()

    def _L0_attn_setup():
        import jax, jax.numpy as jnp
        import numpy as np
        NUM_HEADS = 16
        MASK_NEG = -66504.0
        key = jax.random.key(seed)
        ks = jax.random.split(key, 5)
        B, S, E = (1, 256, 256)
        return {'hidden_states': jax.random.normal(ks[0], (B, S, E), dtype=jnp.float32), 'q_wei': jax.random.normal(ks[1], (E, E), dtype=jnp.float32) * E ** (-0.5), 'k_wei': jax.random.normal(ks[2], (E, E), dtype=jnp.float32) * E ** (-0.5), 'v_wei': jax.random.normal(ks[3], (E, E), dtype=jnp.float32) * E ** (-0.5), 'out_wei': jax.random.normal(ks[4], (E, E), dtype=jnp.float32) * E ** (-0.5)}
    _L0_attn_all = _L0_attn_setup()
    _L0_attn_in = {k: v for k, v in _L0_attn_all.items() if k in ('q_wei', 'k_wei', 'v_wei', 'out_wei')}
    del _L0_attn_all

    def _L0_xattn_setup():
        import jax, jax.numpy as jnp
        import numpy as np
        NUM_HEADS = 16

        def _qdq(x):
            s = jnp.maximum(jnp.max(jnp.abs(x), axis=-1, keepdims=True) / 127.0, 1e-08)
            return jnp.clip(jnp.round(x / s), -127.0, 127.0) * s
        key = jax.random.key(seed)
        ks = jax.random.split(key, 8)
        B, N, M, D = (2, 512, 64, 256)
        w_std = 0.02
        return {'x': jax.random.normal(ks[0], (B, N, D), jnp.float32), 'cond': jax.random.normal(ks[1], (B, M, D), jnp.float32), 'wq': jax.random.normal(ks[2], (D, D), jnp.float32) * w_std, 'bq': jax.random.normal(ks[3], (D,), jnp.float32) * w_std, 'wkv': jax.random.normal(ks[4], (2 * D, D), jnp.float32) * w_std, 'bkv': jax.random.normal(ks[5], (2 * D,), jnp.float32) * w_std, 'wp': jax.random.normal(ks[6], (D, D), jnp.float32) * w_std, 'bp': jax.random.normal(ks[7], (D,), jnp.float32) * w_std}
    _L0_xattn_all = _L0_xattn_setup()
    _L0_xattn_in = {k: v for k, v in _L0_xattn_all.items() if k in ('wq', 'bq', 'wkv', 'bkv', 'wp', 'bp')}
    del _L0_xattn_all

    def _L0_ffn_setup():
        import jax, jax.numpy as jnp
        import numpy as np
        B, S, D = (4, 128, 256)
        H = 512
        NE = 8
        TOPK = 2
        key = jax.random.key(seed)
        ks = jax.random.split(key, 9)
        s = lambda fan_in: 1.0 / np.sqrt(fan_in)
        return {'x': jax.random.normal(ks[0], (B, S, D), dtype=jnp.float32), 'W1': jax.random.normal(ks[1], (NE, D, H), dtype=jnp.float32) * s(D), 'b1': jnp.zeros((NE, H), dtype=jnp.float32), 'W2': jax.random.normal(ks[2], (NE, H, H), dtype=jnp.float32) * s(H), 'b2': jnp.zeros((NE, H), dtype=jnp.float32), 'W3': jax.random.normal(ks[3], (NE, H, D), dtype=jnp.float32) * s(H), 'b3': jnp.zeros((NE, D), dtype=jnp.float32), 'Wg': jax.random.normal(ks[4], (D, NE), dtype=jnp.float32) * s(D), 'bg': jnp.zeros((NE,), dtype=jnp.float32)}
    _L0_ffn_all = _L0_ffn_setup()
    _L0_ffn_in = {k: v for k, v in _L0_ffn_all.items() if k in ('W1', 'b1', 'W2', 'b2', 'W3', 'b3', 'Wg', 'bg')}
    del _L0_ffn_all
    return {'x': x, 'ctx_2048': ctx_2048, 'L0_attn_q_wei': _L0_attn_in['q_wei'], 'L0_attn_k_wei': _L0_attn_in['k_wei'], 'L0_attn_v_wei': _L0_attn_in['v_wei'], 'L0_attn_out_wei': _L0_attn_in['out_wei'], 'L0_xattn_wq': _L0_xattn_in['wq'], 'L0_xattn_bq': _L0_xattn_in['bq'], 'L0_xattn_wkv': _L0_xattn_in['wkv'], 'L0_xattn_bkv': _L0_xattn_in['bkv'], 'L0_xattn_wp': _L0_xattn_in['wp'], 'L0_xattn_bp': _L0_xattn_in['bp'], 'L0_ffn_W1': _L0_ffn_in['W1'], 'L0_ffn_b1': _L0_ffn_in['b1'], 'L0_ffn_W2': _L0_ffn_in['W2'], 'L0_ffn_b2': _L0_ffn_in['b2'], 'L0_ffn_W3': _L0_ffn_in['W3'], 'L0_ffn_b3': _L0_ffn_in['b3'], 'L0_ffn_Wg': _L0_ffn_in['Wg'], 'L0_ffn_bg': _L0_ffn_in['bg']}

def reference(x, ctx_2048, L0_attn_q_wei, L0_attn_k_wei, L0_attn_v_wei, L0_attn_out_wei, L0_xattn_wq, L0_xattn_bq, L0_xattn_wkv, L0_xattn_bkv, L0_xattn_wp, L0_xattn_bp, L0_ffn_W1, L0_ffn_b1, L0_ffn_W2, L0_ffn_b2, L0_ffn_W3, L0_ffn_b3, L0_ffn_Wg, L0_ffn_bg):
    import jax
    import jax.numpy as jnp

    def _L0_attn_ref(hidden_states, q_wei, k_wei, v_wei, out_wei):
        import jax, jax.numpy as jnp
        import numpy as np
        NUM_HEADS = 16
        MASK_NEG = -66504.0
        B, S, E = hidden_states.shape
        H = NUM_HEADS
        D = E // H
        q = hidden_states @ q_wei
        k = hidden_states @ k_wei
        v = hidden_states @ v_wei
        q = q.reshape(B, S, H, D).transpose(0, 2, 1, 3)
        k = k.reshape(B, S, H, D).transpose(0, 2, 1, 3)
        v = v.reshape(B, S, H, D).transpose(0, 2, 1, 3)
        scores = jnp.einsum('bhqd,bhkd->bhqk', q, k)
        causal = jnp.triu(jnp.full((S, S), MASK_NEG, dtype=scores.dtype), k=1)
        scores = scores + causal[None, None]
        scores = scores / jnp.sqrt(jnp.asarray(D, dtype=scores.dtype))
        probs = jax.nn.softmax(scores.astype(jnp.float32), axis=-1).astype(q.dtype)
        attn = jnp.einsum('bhqk,bhkd->bhqd', probs, v)
        attn = attn.transpose(0, 2, 1, 3).reshape(B, S, E)
        return attn @ out_wei

    def _L0_xattn_ref(x, cond, wq, bq, wkv, bkv, wp, bp):
        import jax, jax.numpy as jnp
        import numpy as np
        NUM_HEADS = 16

        def _qdq(x):
            s = jnp.maximum(jnp.max(jnp.abs(x), axis=-1, keepdims=True) / 127.0, 1e-08)
            return jnp.clip(jnp.round(x / s), -127.0, 127.0) * s
        B, N, C = x.shape
        M = cond.shape[1]
        H = NUM_HEADS
        Dh = C // H
        q = _qdq(x) @ _qdq(wq).T + bq
        kv = cond @ wkv.T + bkv
        k, v = jnp.split(kv, 2, axis=-1)
        q = q.reshape(B, N, H, Dh)
        k = k.reshape(B, M, H, Dh)
        v = v.reshape(B, M, H, Dh)
        scale = 1.0 / np.sqrt(Dh)
        attn = jax.nn.softmax(jnp.einsum('bnhd,bmhd->bhnm', q, k) * scale, axis=-1)
        o = jnp.einsum('bhnm,bmhd->bnhd', attn, v).reshape(B, N, C)
        out = _qdq(o) @ _qdq(wp).T + bp
        return out

    def _L0_ffn_ref(x, W1, b1, W2, b2, W3, b3, Wg, bg):
        import jax, jax.numpy as jnp
        import numpy as np
        B, S, D = (4, 128, 256)
        H = 512
        NE = 8
        TOPK = 2
        gate_logits = jnp.einsum('bsd,dn->bsn', x, Wg) + bg
        gate_weights = jax.nn.softmax(gate_logits, axis=-1)
        topv, topi = jax.lax.top_k(gate_weights, TOPK)
        h = jax.nn.gelu(jnp.einsum('bsd,ndh->nbsh', x, W1) + b1[:, None, None, :], approximate=False)
        h = jax.nn.gelu(jnp.einsum('nbsh,nhf->nbsf', h, W2) + b2[:, None, None, :], approximate=False)
        eo = jnp.einsum('nbsf,nfd->nbsd', h, W3) + b3[:, None, None, :]
        comb = jnp.sum(jax.nn.one_hot(topi, NE, dtype=x.dtype) * topv[..., None], axis=-2)
        out = jnp.einsum('nbsd,bsn->bsd', eo, comb)
        return out
    x = _layernorm(x + _L0_attn_ref(x, L0_attn_q_wei, L0_attn_k_wei, L0_attn_v_wei, L0_attn_out_wei), axis=-1)
    x = _layernorm(x + _L0_xattn_ref(x, ctx_2048, L0_xattn_wq, L0_xattn_bq, L0_xattn_wkv, L0_xattn_bkv, L0_xattn_wp, L0_xattn_bp), axis=-1)
    x = _layernorm(x + _L0_ffn_ref(x, L0_ffn_W1, L0_ffn_b1, L0_ffn_W2, L0_ffn_b2, L0_ffn_W3, L0_ffn_b3, L0_ffn_Wg, L0_ffn_bg), axis=-1)
    return x

_drawn_inputs = setup_inputs


def setup_inputs(seed=0):
    import zlib

    import numpy as np

    out = dict(_drawn_inputs(seed))
    spreads = {'L0_ffn_b1': (0.0, 0.445),
     'L0_ffn_b2': (0.0, 0.301),
     'L0_ffn_b3': (0.0, 0.1),
     'L0_ffn_bg': (0.0, 0.1)}
    factors = {'L0_xattn_wq': 21.396, 'L0_xattn_bq': 200.0, 'L0_xattn_bkv': 6.856}
    for name, (base, spread) in spreads.items():
        noise = np.random.default_rng([zlib.crc32(name.encode()), seed]).standard_normal(out[name].shape)
        drawn = base * np.exp(spread * noise) if base else spread * noise
        out[name] = jnp.asarray(drawn.astype(out[name].dtype))
    for name, factor in factors.items():
        out[name] = (out[name] * factor).astype(out[name].dtype)
    return out
```

```python
import concourse.bass as bass
from concourse import mybir
from contextlib import ExitStack

F32 = mybir.dt.float32
BF16 = mybir.dt.bfloat16
I32 = mybir.dt.int32
U32 = mybir.dt.uint32
ALU = mybir.AluOpType
ACT = mybir.ActivationFunctionType
X = mybir.AxisListType.X

B, S, D, H, DH = 4, 256, 256, 16, 16
SK = 1601
P = 128
NT = B * S // P
HH = H // 2
UH = 4
PARTS = 3
Q_PARTS = (0, 1, 2, 0, 1, 0)
K_PARTS = (0, 0, 0, 1, 1, 2)
NPROD = len(Q_PARTS)
MROW = NPROD * DH
STACK = MROW + PARTS
VW = DH + 1
NE, FH = 8, 512
WE = (D * FH + FH * FH + FH * D) // P
BE = FH + FH + D
TILES = 2 * B * S // P + NE
MASK = -66504.0
EPS = 1e-5
ROUND = 12582912.0
M_RING, ST_RING, PROB_RING = 3, 2, 4


def NS(**named):
    return type("Named", (), named)


class Tally:

    def __init__(self, sem, per_turn=0, credit=0):
        self.sem, self.per_turn, self.credit, self.n = sem, per_turn, credit, 0
        self.turn, self.start = 0, None

    def loop(self, turn):
        if self.start is None:
            self.start = self.n
        else:
            assert self.n == self.start + self.per_turn, (self.sem, self.n - self.start, self.per_turn)
        self.n, self.turn = self.start, turn

    def value(self, more=0):
        return self.turn * self.per_turn + (self.n + more)

    def done(self, more=0):
        return self.turn * self.per_turn + (self.n + more + self.credit)


def self_attention_shape():
    c = NS(name="sa", cross=False, T=S, tiles=[P] * (S // P), chunks=[(0, S)])
    c.groups = [[0, 1]]
    return c


def cross_attention_shape():
    c = NS(name="xa", cross=True, T=SK, tiles=[P] * (SK // P) + [SK % P])
    w = -(-SK // 4)
    c.chunks = [(i * 400 + min(i, 1), 401 if i == 0 else 400) for i in range(4)]
    assert c.chunks[-1][0] + c.chunks[-1][1] == SK and w <= 512
    c.groups = [list(range(i, min(i + 4, len(c.tiles)))) for i in range(0, len(c.tiles), 4)]
    return c


def finish_shape(c):
    c.NC = len(c.chunks)
    c.vjobs = -(-len(c.tiles) // 4)
    c.kq_jobs = (1 + c.cross, 1)
    unit = 2 * UH * c.NC
    step = 3 + unit
    c.setup_jobs = 2 if c.cross else 0
    c.m_k = (c.setup_jobs + c.kq_jobs[0], c.setup_jobs + c.kq_jobs[0] + c.vjobs + 1)
    c.m_v1 = c.m_k[1] + unit + c.vjobs
    c.m_before = c.m_v1 + 2 + unit
    jobs = sum(c.kq_jobs) + 2 * c.vjobs + 4 * step + 2
    c.pad = -jobs % M_RING
    c.m_turn = jobs + c.pad
    c.m_turn_k = (c.kq_jobs[0], c.kq_jobs[0] + 2 * step + c.vjobs + 1)
    c.kjobs = 2 if c.cross else 0
    c.st_unit = UH * len(c.groups)
    c.st_before = 2 * c.kjobs + c.st_unit
    c.st_turn = 2 * c.kjobs + 4 * c.st_unit
    c.pv_turn = 4 * c.st_unit
    return c


def m_after_qk(c, b, m):
    if isinstance(b, int) and b == 0:
        return M_RING + c.m_k[m]
    return M_RING + c.m_before + (b - 1) * c.m_turn + c.m_turn_k[m]


def attention_sems(ctx, nc, c):
    names = ("m_full m_free st_full act_done o_free pv_done mparts_ready w_ready xq_ready oq_ready masked parts_ready "
             "scratch_written stack0_loaded stack1_loaded x_loaded var_ready rstd_ready dve_chain pool_chain turnstile")
    return NS(**{n: ctx.enter_context(nc.semaphore(f"{c.name}_{n}")) for n in names.split()})



def pe_attention(nc, pe, c, s, t):
    mt = Tally(s.m_free, c.m_turn, M_RING)
    st = Tally(s.act_done, c.st_turn, ST_RING)
    ot = Tally(s.o_free, 4, 1)
    pt = Tally(s.pv_done, c.pv_turn, PROB_RING)
    mp = Tally(s.mparts_ready, 4, 0)

    def m_bank():
        pe.wait_ge(mt.sem, mt.value(1))
        return t.mbank[mt.n % M_RING]

    def m_done(last, n=1):
        last.then_inc(s.m_full, n)
        mt.n += n

    def m_drained():
        pe.wait_ge(mt.sem, mt.done())

    def transposes(src, ready=None):
        bank = m_bank()
        if ready is not None:
            pe.wait_ge(*ready)
        for tt in range(2):
            for k in range(2):
                last = nc.tensor.transpose(bank[:, (2 * k + tt) * P:(2 * k + tt + 1) * P],
                                           src[:, tt, k * P:(k + 1) * P], t.ident[:, :])
        m_done(last)

    def project_qk(b, m):
        pe.wait_ge(s.x_loaded, b * 16 + 16)
        ms = slice(m * P, (m + 1) * P)
        for pair in ((0, 1), (2, 3))[:c.kjobs]:
            pe.wait_ge(st.sem, st.value(1))
            bank = t.stbank[st.n % ST_RING]
            for i, ch in enumerate(pair):
                a, w = c.chunks[ch]
                for k in range(2):
                    last = nc.tensor.matmul(bank[:, i * 512:i * 512 + w], t.wk[:, k, ms], t.xT[:, k, a:a + w],
                                            start=(k == 0), stop=(k == 1))
            last.then_inc(s.st_full, 1)
            st.n += 1
        if c.cross and m == 0:
            transposes(t.xq, (s.xq_ready, b + 1))
            m_drained()
        bank = m_bank()
        for k in range(2):
            rhs = t.xqT[:, k, :] if c.cross else t.xT[:, k, :]
            last = nc.tensor.matmul(bank[:, 0:S], t.wq[:, k, ms], rhs, start=(k == 0), stop=(k == 1))
        if not c.cross:
            for k in range(2):
                last = nc.tensor.matmul(bank[:, S:2 * S], t.wk[:, k, ms], t.xT[:, k, :], start=(k == 0), stop=(k == 1))
        m_done(last)

    def project_v(m):
        for v in range(c.vjobs):
            bank = m_bank()
            for i, kt in enumerate(range(4 * v, min(4 * v + 4, len(c.tiles)))):
                n = c.tiles[kt]
                for k in range(2):
                    last = nc.tensor.matmul(bank[0:n, i * P:(i + 1) * P], t.xT[:, k, kt * P:kt * P + n],
                                            t.wv[:, k, m * P:(m + 1) * P], start=(k == 0), stop=(k == 1))
            m_done(last)

    def stack_loaded(b, m):
        pe.wait_ge((s.stack0_loaded, s.stack1_loaded)[m], b * 192 + 192)

    def max_jobs(unit):
        m, g = unit
        for j in range(UH):
            h = UH * g + j
            for qt in range(2):
                for a, w in c.chunks:
                    bank = m_bank()
                    m_done(nc.tensor.matmul(bank[:, 0:w], t.qst[m][0:MROW, h, qt * P:(qt + 1) * P],
                                            t.kst[m][0:MROW, h, a:a + w], start=True, stop=True))
                    yield

    def pv(unit, j, grp, n_st, first, final):
        m, g = unit
        h = UH * g + j
        if first:
            pe.wait_ge(ot.sem, ot.value(1))
        if c.cross:
            pe.wait_ge(s.act_done, st.turn * c.st_turn + (n_st + 1 + ST_RING))
        else:
            pe.wait_ge(s.masked, pt.value(1))
        slot = t.probs[pt.n % PROB_RING]
        for i, kt in enumerate(grp):
            n = c.tiles[kt]
            last = nc.tensor.matmul(t.obank[32 * j:32 * j + VW, 0:S], t.vaug[m][0:n, kt, h, :],
                                    slot[0:n, i * S:(i + 1) * S], start=(kt == 0), stop=(kt == len(c.tiles) - 1))
        last.then_inc(s.pv_done, 1)
        pt.n += 1
        if final:
            ot.n += 1

    def o_transposes():
        bank = m_bank()
        pe.wait_ge(ot.sem, ot.done())
        for qt in range(2):
            last = nc.tensor.transpose(bank[:, qt * P:(qt + 1) * P], t.oT_unit[:, qt * P:(qt + 1) * P], t.ident[:, :])
        m_done(last)

    def step(unit, nxt, pending, output_of=None):
        m, g = unit
        pe.wait_ge(mp.sem, mp.value(1))
        mp.n += 1
        for jb in range(2):
            bank = m_bank()
            for u in range(4):
                last = nc.tensor.matmul(bank[MROW:STACK, u * P:(u + 1) * P], t.mparts[:, 4 * jb + u, :], t.ident_bf[:, :],
                                        start=True, stop=True)
            m_done(last)
        m_drained()
        more = max_jobs(nxt) if nxt else iter(())
        late = None
        for j in range(UH):
            h = UH * g + j
            for gi, grp in enumerate(c.groups):
                pe.wait_ge(st.sem, st.value(1))
                bank = t.stbank[st.n % ST_RING]
                for i, kt in enumerate(grp):
                    n = c.tiles[kt]
                    last = nc.tensor.matmul(bank[0:n, i * S:(i + 1) * S], t.kst[m][0:STACK, h, kt * P:kt * P + n],
                                            t.qst[m][0:STACK, h, :], start=True, stop=True)
                last.then_inc(s.st_full, 1)
                this = (j, grp, st.n, j == 0 and gi == 0, False)
                st.n += 1
                for _ in range(2):
                    next(more, None)
                if late:
                    pv(unit, *late)
                late = this
            if j == 0 and pending:
                o_transposes()
            if j == 2 and output_of is not None:
                output_transposes(output_of)
        for _ in more:
            pass
        pv(unit, *late[:4], True)
        if output_of is not None:
            output_product()

    def output_transposes(b):
        if c.cross:
            transposes(t.oq, (s.oq_ready, b + 1))
        else:
            m_drained()
            transposes(t.o_tm)

    def output_product():
        m_drained()
        bank = m_bank()
        for tt in range(2):
            for k in range(2):
                last = nc.tensor.matmul(bank[:, tt * D:(tt + 1) * D], t.oT[:, k, tt * P:(tt + 1) * P], t.wo[:, k, :],
                                        start=(k == 0), stop=(k == 1))
        m_done(last, 1 + c.pad)

    def body(b, last):
        for x in (mt, st, ot, pt, mp):
            x.loop(b)
        if not last:
            project_qk(b + 1, 0)
        stack_loaded(b, 1)
        step((0, 1), (1, 0), True)
        if not last:
            project_v(0)
        step((1, 0), (1, 1), True)
        if last:
            step((1, 1), None, True)
            o_transposes()
            output_transposes(b)
            output_product()
        else:
            project_qk(b + 1, 1)
            stack_loaded(b + 1, 0)
            step((1, 1), (0, 0), True)
            project_v(1)
            step((0, 0), (0, 1), True, output_of=b)

    pe.sem_inc(s.pv_done, PROB_RING)
    if c.cross:
        transposes(t.wq_q, (s.w_ready, 1))
        transposes(t.wp_q, (s.w_ready, 2))
        m_drained()
    project_qk(0, 0)
    project_v(0)
    project_qk(0, 1)
    stack_loaded(0, 0)
    for _ in max_jobs((0, 0)):
        pass
    project_v(1)
    step((0, 0), (0, 1), False)
    with pe.Fori(0, B - 1) as b:
        body(b, False)
    body(B - 1, True)



def dve_attention(nc, dve, c, s, t):
    V = nc.vector
    mt = Tally(s.m_full, c.m_turn)
    ot = Tally(s.pv_done, c.pv_turn, PROB_RING)
    ch = Tally(s.dve_chain, c.chain_turn)

    def link(ins, plain=False):
        ins.then_inc(s.dve_chain, 1)
        ch.n += 1
        dve.wait_ge(ch.sem, ch.value())
        if plain:
            dve.sem_inc(s.turnstile, 1)

    def job(plain=False):
        dve.wait_ge(mt.sem, mt.value(1))
        if plain:
            dve.sem_inc(s.turnstile, 1)
        return t.mbank[mt.n % M_RING]

    def free(ins, n=1):
        ins.then_inc(s.m_free, n)
        mt.n += n

    def settled():
        dve.wait_ge(s.m_free, mt.value() + M_RING)

    def quantise(src, dst, ready):
        for _ in quantise_steps(src, dst, ready):
            pass

    def quantise_steps(src, dst, ready):
        link(V.tensor_reduce(t.qs[:, 0, :], src, X, ALU.max, apply_absolute_value=True))
        yield
        link(V.tensor_scalar(t.qs[:, 1, :], t.qs[:, 0, :], 1.0 / 127.0, 1e-8, ALU.mult, ALU.max))
        yield
        link(V.reciprocal(t.qs[:, 2, :], t.qs[:, 1, :]))
        yield
        scale, inverse = (t.qs[:, i, :].unsqueeze(2).to_broadcast([P, 2, D]) for i in (1, 2))
        link(V.tensor_tensor(t.qa[:, :, :], src, inverse, ALU.mult))
        yield
        link(V.tensor_scalar(t.qb[:, :, :], t.qa[:, :, :], ROUND, -ROUND, ALU.add, ALU.add))
        yield
        link(V.tensor_scalar(t.qa[:, :, :], t.qb[:, :, :], 127.0, -127.0, ALU.min, ALU.max))
        yield
        V.tensor_tensor(dst, t.qa[:, :, :], scale, ALU.mult).then_inc(ready, 1)

    def take_transposed(dst):
        bank = job()
        free(V.tensor_copy(dst.rearrange("p k t -> p (k t)"), bank[:, 0:2 * D]))

    def take_qk(b, m):
        if c.cross and m == 0:
            if not (isinstance(b, int) and b == 0):
                dve.wait_ge(s.xq_ready, b)
            quantise(t.x_in[:, bass.ds(2 * b, 2), :], t.xq[:, :, :], s.xq_ready)
            take_transposed(t.xqT)
        bank = job()
        if not (isinstance(b, int) and b == 0 and m == 0):
            dve.wait_ge(s.parts_ready, 2 * b + m)
        if c.cross:
            free(V.tensor_scalar(t.f[:, 0:S], bank[:, 0:S], t.bq[:, m:m + 1], None, ALU.add))
        else:
            free(V.tensor_copy(t.f[:, 0:2 * S], bank[:, 0:2 * S]))

    def take_v(m):
        for v in range(c.vjobs):
            tiles = c.tiles[4 * v:4 * v + 4]
            n, k = tiles[0], len(tiles)
            bank = job()
            src = bank[0:n, 0:k * P].rearrange("p (k h d) -> p k h d", k=k, h=HH)
            dst = t.vaug[m][0:n, 4 * v:4 * v + k, :, 0:DH]
            if c.cross:
                for i in range(k):
                    bias = t.bv[0:n, m * P:(m + 1) * P].rearrange("p (h d) -> p h d", h=HH)
                    ins = V.tensor_tensor(dst[:, i], src[:, i], bias, ALU.add)
                free(ins)
            else:
                free(V.tensor_copy(dst, src))

    def max_jobs(unit):
        settled()
        for u in range(2 * UH):
            for i, (a, w) in enumerate(c.chunks):
                bank = job(plain=not c.cross)
                if c.cross:
                    free(V.reduce_max(t.mx[:, u, i:i + 1], bank[:, 0:w], X))
                else:
                    free(V.tensor_tensor_reduce(out=t.junk[:, u, :], in0=bank[:, 0:S], in1=t.cmask[:, u % 2, :],
                                                scale=1.0, scalar=-3.0e38, op0=ALU.add, op1=ALU.max,
                                                accum_out=t.mx[:, u, i:i + 1]))
                yield

    def max_rows():
        settled()
        link(V.tensor_reduce(t.nm[:, 0, :], t.mx[:, :, :], X, ALU.max, negate=True))
        link(V.tensor_copy(t.mparts[:, :, 0], t.nm[:, 0, :]))
        link(V.tensor_tensor(t.nm[:, 1, :], t.nm[:, 0, :], t.mparts[:, :, 0], ALU.subtract))
        link(V.tensor_copy(t.mparts[:, :, 1], t.nm[:, 1, :]))
        V.tensor_tensor(t.mparts[:, :, 2], t.nm[:, 1, :], t.mparts[:, :, 1], ALU.subtract).then_inc(s.mparts_ready, 1)

    def copy_o():
        ot.n += c.st_unit
        dve.wait_ge(ot.sem, ot.done())
        V.tensor_copy(t.oT_unit[:, :], t.obank[:, 0:S]).then_inc(s.o_free, 1)

    def take_o(unit):
        m, g = unit
        bank = job()
        v = bank[:, 0:2 * P].rearrange("p (q j w) -> p q j w", q=2, j=UH)
        settled()
        link(V.reciprocal(t.rden[:, :, :], v[:, :, :, DH]))
        a = (m * HH + g * UH) * DH
        dst = t.o_tm[:, :, a:a + UH * DH].rearrange("p q (j d) -> p q j d", j=UH)
        free(V.tensor_tensor(dst, v[:, :, :, 0:DH], t.rden[:, :, :].unsqueeze(3).to_broadcast([P, 2, UH, DH]), ALU.mult))

    def step(unit, nxt, pending, output_of=None):
        m, g = unit
        for jb in range(2):
            bank = job()
            h = UH * g + 2 * jb
            free(V.tensor_copy(t.qst[m][MROW:STACK, h:h + 2, :],
                               bank[MROW:STACK, 0:2 * S].rearrange("p (h q) -> p h q", h=2)))
        more = max_jobs(nxt) if nxt else iter(())
        for _ in range(2 * len(c.groups)):
            next(more, None)
        if pending:
            take_o(pending)
        if output_of is not None:
            between = iter(())
            if c.cross:
                settled()
                between = quantise_steps(t.o_tm[:, :, :], t.oq[:, :, :], s.oq_ready)
            for n in range(2 * 2 * len(c.groups)):
                next(more)
                if n % 2 == 0:
                    next(between, None)
            for _ in between:
                pass
            take_transposed(t.oT)
        for _ in more:
            pass
        if nxt:
            max_rows()
        copy_o()
        if output_of is not None:
            take_output(output_of)

    def take_output(b):
        bank = job()
        out = bank[:, 0:2 * D].rearrange("p (q d) -> p q d", q=2)
        free(V.tensor_tensor(t.y[:, :, :], out, t.x_in[:, bass.ds(2 * b, 2), :], ALU.add), 1 + c.pad)
        settled()
        y = t.y
        if c.cross:
            link(V.tensor_tensor(t.y2[:, :, :], t.y[:, :, :], t.bp[:, :].unsqueeze(1).to_broadcast([P, 2, D]), ALU.add))
            y = t.y2
        for q in range(2):
            ins = V.bn_stats(t.stats[:, q, :], y[:, q, :])
        link(ins, plain=True)
        for q in range(2):
            ins = V.bn_aggr(t.mv[:, q, :], t.stats[:, q, :])
        link(ins)
        V.tensor_scalar(t.ve[:, :], t.mv[:, :, 1], EPS, None, ALU.add).then_inc(s.var_ready, 1)
        dve.wait_ge(s.rstd_ready, b + 1)
        for q in range(2):
            ins = V.tensor_scalar(t.x_out[:, 2 * b + q, :], y[:, q, :], t.mv[:, q, 0:1], t.rstd[:, q:q + 1],
                                  ALU.subtract, ALU.mult)
        link(ins)

    def body(b, last):
        for x in (mt, ot, ch):
            x.loop(b)
        if not last:
            take_qk(b + 1, 0)
        step((0, 1), (1, 0), (0, 0))
        if not last:
            take_v(0)
        step((1, 0), (1, 1), (0, 1))
        if last:
            step((1, 1), None, (1, 0))
            take_o((1, 1))
            if c.cross:
                settled()
                quantise(t.o_tm[:, :, :], t.oq[:, :, :], s.oq_ready)
            take_transposed(t.oT)
            take_output(b)
        else:
            take_qk(b + 1, 1)
            step((1, 1), (0, 0), (1, 0))
            take_v(1)
            step((0, 0), (0, 1), (1, 1), output_of=b)

    dve.sem_inc(s.m_free, M_RING)
    dve.sem_inc(s.o_free, 1)
    if c.cross:
        dve.wait_ge(t.loaded, t.loaded_all)
        quantise(t.wq_raw[:, :, :], t.wq_q[:, :, :], s.w_ready)
        quantise(t.wp_raw[:, :, :], t.wp_q[:, :, :], s.w_ready)
        take_transposed(t.wq)
        take_transposed(t.wo)
    take_qk(0, 0)
    take_v(0)
    take_qk(0, 1)
    for _ in max_jobs((0, 0)):
        pass
    max_rows()
    take_v(1)
    step((0, 0), (0, 1), None)
    with dve.Fori(0, B - 1) as b:
        body(b, False)
    body(B - 1, True)



def act_attention(nc, act, c, s, t):
    st = Tally(s.st_full, c.st_turn)
    pt = Tally(s.pv_done, c.pv_turn, PROB_RING)

    def take_k(b, m):
        for pair in ((0, 1), (2, 3))[:c.kjobs]:
            act.wait_ge(st.sem, st.value(1))
            if not (isinstance(b, int) and b == 0 and m == 0):
                act.wait_ge(s.parts_ready, 2 * b + m)
            bank = t.stbank[st.n % ST_RING]
            for i, chunk in enumerate(pair):
                a, w = c.chunks[chunk]
                last = nc.scalar.activation(t.f[:, S + a:S + a + w], bank[:, i * 512:i * 512 + w], ACT.Identity,
                                            bias=t.bk[:, m:m + 1])
            last.then_inc(s.act_done, 1)
            st.n += 1

    def step():
        for j in range(UH):
            for grp in c.groups:
                act.wait_ge(st.sem, st.value(1))
                act.wait_ge(pt.sem, pt.value(1))
                n = c.tiles[grp[0]]
                w = len(grp) * S
                nc.scalar.activation(t.probs[pt.n % PROB_RING][0:n, 0:w], t.stbank[st.n % ST_RING][0:n, 0:w],
                                     ACT.Exp, scale=float(DH) ** -0.5).then_inc(s.act_done, 1)
                st.n += 1
                pt.n += 1

    def body(b, last):
        for x in (st, pt):
            x.loop(b)
        if not last:
            take_k(b + 1, 0)
        step()
        step()
        if not last:
            take_k(b + 1, 1)
        step()
        if not last:
            step()

    act.sem_inc(s.act_done, ST_RING)
    if c.cross:
        act.wait_ge(t.loaded, t.loaded_all)
    take_k(0, 0)
    take_k(0, 1)
    step()
    with act.Fori(0, B - 1) as b:
        body(b, False)
    body(B - 1, True)



def pool_attention(nc, pool, c, s, t):
    G = nc.gpsimd
    st = Tally(s.act_done, c.st_turn, ST_RING)
    ch = Tally(s.pool_chain, 6)
    pt = Tally(None, c.pv_turn)

    def link(ins, plain=False):
        ins.then_inc(s.pool_chain, 1)
        ch.n += 1
        pool.wait_ge(ch.sem, ch.value())
        if plain:
            pool.sem_inc(s.turnstile, 1)

    def split(b, m):
        pool.wait_ge(s.m_free, m_after_qk(c, b, m))
        if c.cross:
            st.n += c.kjobs
            pool.wait_ge(st.sem, st.done())
        if not (isinstance(b, int) and b == 0 and m == 0):
            pool.wait_ge(s.scratch_written, 32 * b + 16 * m)
        pool.sem_inc(s.turnstile, 1)
        link(G.tensor_copy(t.parts[:, 0, :], t.f[:, :]))
        link(G.tensor_tensor(t.f[:, :], t.f[:, :], t.parts[:, 0, :], ALU.subtract), plain=True)
        link(G.tensor_copy(t.parts[:, 1, :], t.f[:, :]))
        G.tensor_tensor(t.parts[:, 2, :], t.f[:, :], t.parts[:, 1, :], ALU.subtract).then_inc(s.parts_ready, 1)

    def step():
        for _ in range(c.st_unit):
            st.n += 1
            if not c.cross:
                pool.wait_ge(st.sem, st.done())
                pool.sem_inc(s.turnstile, 1)
                slot = t.probs[pt.n % PROB_RING][:, 0:2 * S].rearrange("p (k q) -> p k q", k=2)
                G.affine_select(out=slot, in_=slot, compare_op=ALU.is_ge, fill=0.0, base=0,
                                pattern=[[-P, 2], [1, S]], channel_multiplier=-1).then_inc(s.masked, 1)
            pt.n += 1

    def body(b, last):
        for x in (st, ch, pt):
            x.loop(b)
        if not last:
            split(b + 1, 0)
        step()
        step()
        if not last:
            split(b + 1, 1)
        step()
        if not last:
            step()
        pool.wait_ge(s.var_ready, b + 1)
        G.tensor_tensor(t.rstd[:, :], t.ve[:, :], t.neg_half[:, :], ALU.pow).then_inc(s.rstd_ready, 1)

    split(0, 0)
    split(0, 1)
    step()
    with pool.Fori(0, B - 1) as b:
        body(b, False)
    body(B - 1, True)



def sp_attention(nc, sp, c, s, t, x_dram, scratch):
    def load_input(b):
        sp.dma_start(t.xT[:, :, :], x_dram[b, :, :].rearrange("(k p) t -> p k t", p=P)).then_inc(s.x_loaded, 16)

    def stacks(b, m, st_done):
        sp.wait_ge(s.parts_ready, 2 * b + (m + 1))
        sp.sem_inc(s.turnstile, 1)
        sems = (s.stack0_loaded, s.stack1_loaded)
        if not (isinstance(b, int) and b == 0):
            sp.wait_ge(sems[m], 192 * b)
        sp.dma_start(scratch[m, :, :, :].rearrange("s f t -> f s t"), t.parts[:, :, :]).then_inc(s.scratch_written, 16)
        sp.wait_ge(s.scratch_written, 32 * b + (16 * m + 16))
        sp.sem_inc(s.turnstile, 1)
        if st_done is not None:
            sp.wait_ge(s.act_done, st_done)
        for i in range(NPROD):
            rows = slice(i * DH, (i + 1) * DH)
            sp.dma_start(t.kst[m][rows, :, 0:c.T], scratch[m, K_PARTS[i], :, S:].rearrange("(j d) t -> d j t", d=DH))\
                .then_inc(sems[m], 16)
            sp.dma_start(t.qst[m][rows, :, :], scratch[m, Q_PARTS[i], :, 0:S].rearrange("(j d) t -> d j t", d=DH))\
                .then_inc(sems[m], 16)

    load_input(0)
    stacks(0, 0, None)
    stacks(0, 1, None)
    with sp.Fori(0, B - 1) as b:
        sp.wait_ge(s.m_free, M_RING + c.m_v1 + b * c.m_turn)
        sp.sem_inc(s.turnstile, 1)
        load_input(b + 1)
        base = ST_RING + c.st_before + b * c.st_turn
        stacks(b + 1, 0, base + (c.kjobs + c.st_unit))
        stacks(b + 1, 1, base + (2 * c.kjobs + 3 * c.st_unit))



def experts_block(nc, a, out, x2, ident, ident_bf):
    ctx = ExitStack()
    with ctx:
        def sb(name, shape, dt=F32):
            return ctx.enter_context(nc.sbuf_tensor(name, shape, dt))

        def sem(name):
            return ctx.enter_context(nc.semaphore(name))

        slots_x = nc.dram_tensor("slots_x", [TILES * P, D], F32, kind="Internal").ap()
        slots_y = nc.dram_tensor("slots_y", [TILES * P, D], F32, kind="Internal").ap()
        w = sb("expert_w", [P, NE * WE])
        bias_raw = sb("bias_raw", [NE, BE])
        bias_split = sb("bias_split", [NE, PARTS, BE], BF16)
        bias = sb("bias_rows", [PARTS, NE * BE], BF16)
        wg, bg = sb("wg", [P, 2, NE]), sb("bg", [P, NE])
        ones, tri = sb("ones_bf", [P, P], BF16), sb("tri_bf", [P, P], BF16)
        zeros = sb("zeros", [P, D])
        x2T = sb("x2T", [P, 2 * NT, P])
        counting = sb("counting", [P, TILES], I32)
        count_f, count_128 = sb("count_f", [P, TILES]), sb("count_128", [P, NE])
        logits, best, away = sb("logits", [P, NT, NE]), sb("best", [P, NT, NE]), sb("away", [P, NT, NE])
        expd, total = sb("expd", [P, NT, NE]), sb("total", [P, 2, NT])
        gate, best_at, best_f = sb("gate", [P, NT, 2]), sb("best_at", [P, NT, NE], U32), sb("best_f", [P, NT, 2])
        hot, both = sb("hot", [P, NT, 2, NE]), sb("both", [P, NT, NE], BF16)
        many, tiles_of = sb("many", [P, NE, NE]), sb("tiles_of", [P, NE])
        end, first = sb("end", [P, NE]), sb("first", [P, NE])
        place, place_hot = sb("place", [P, NT, NE]), sb("place_hot", [P, NT, 2, NE])
        slot_f, slot = sb("slot_f", [P, NT, 2]), sb("slot", [P, NT, 2], U32)
        past, expert_f, expert = sb("past", [P, TILES, NE]), sb("expert_f", [P, 2, TILES]), sb("expert", [P, TILES], I32)
        ones_ne = sb("ones_ne", [P, NE])
        gathered = w[:, 0:NT * 2 * D].rearrange("p (t c d) -> p t c d", t=NT, c=2)
        y, stats, mv = x2T[:, :, :].rearrange("p (t k) q -> p t (k q)", k=2), sb("stats_c", [P, NT, 6]), sb("mv_c", [P, NT, 2])
        ve, rstd, neg_half = sb("ve_c", [P, NT]), sb("rstd_c", [P, NT]), sb("neg_half_c", [P, NT])
        lane = [NS(xt=sb(f"xt{i}", [P, D]), xT=sb(f"xT_{i}", [P, 2, P]), h=sb(f"h{i}", [P, FH]),
                   hT=[sb(f"h{l}T_{i}", [P, FH // P, P]) for l in (1, 2)], y=sb(f"y_{i}", [P, D]),
                   bt=ctx.enter_context(nc.psum_tensor(f"bt{i}", [P, 512], F32)),
                   bh=ctx.enter_context(nc.psum_tensor(f"bh{i}", [P, 512], F32)),
                   by=ctx.enter_context(nc.psum_tensor(f"by{i}", [P, 512], F32)),
                   pe=sem(f"lane{i}_pe"), dve=sem(f"lane{i}_dve"), act=sem(f"lane{i}_act"),
                   x_in=sem(f"lane{i}_x_in"), y_out=sem(f"lane{i}_y_out")) for i in range(2)]
        route = ctx.enter_context(nc.psum_tensor("route", [P, 512], F32))
        x_banks = [lane[0].bt, lane[0].bh, lane[1].bt, lane[1].bh]
        small, weights, made, zeroed = sem("small_in"), [sem(f"w{e}_in") for e in range(NE)], sem("made_c"), sem("zeroed")
        bias_done, bias_in, pe_r, chain = sem("bias_done"), sem("bias_in"), sem("pe_route"), sem("chain_c")
        exp_done, routed, scattered, got = sem("exp_done"), sem("routed"), sem("scattered"), sem("gathered_in")
        var_ready, rstd_ready, final, stored = sem("var_c"), sem("rstd_c_ready"), sem("final"), sem("stored")
        hot_ready, away_ready = sem("hot_ready"), sem("away_ready")
        MADE = 6
        block = ctx.enter_context(nc.Block())

        @block.sync
        def _(sp):
            for dst, src in ((wg[:, :, :], a["wg"].rearrange("(k p) e -> p k e", p=P)), (bg[:, :], a["bg"].partition_broadcast(P)),
                             (bias_raw[:, :], a["bias"])):
                sp.dma_start(dst, src).then_inc(small, 16)
            sp.wait_ge(made, MADE)
            sp.dma_start(slots_x.rearrange("(s p) d -> p s d", p=P),
                         zeros[:, :].unsqueeze(1).to_broadcast([P, TILES, D])).then_inc(zeroed, 16)
            for e in range(NE):
                at = 0
                for name, k, n in (("W1", D // P, FH), ("W2", FH // P, FH), ("W3", FH // P, D)):
                    sp.dma_start(w[:, e * WE + at:e * WE + at + k * n].rearrange("p (k n) -> p k n", k=k),
                                 a[name][e, :, :].rearrange("(k p) n -> p k n", p=P)).then_inc(weights[e], 16)
                    at += k * n
                if e == 0:
                    sp.wait_ge(bias_done, 4)
                    for i in range(PARTS):
                        sp.dma_start(bias[i:i + 1, :], bias_split[:, i, :]).then_inc(bias_in, 16)
            sp.wait_ge(scattered, 16 * 2 * NT)

            def load(l, s):
                sp.dma_start(l.xt[:, :], slots_x[bass.ds(s * P, P), :]).then_inc(l.x_in, 16)

            def store(l, s, i):
                sp.wait_ge(l.dve, 4 * i + (4 + 4))
                sp.sem_inc(stored, 1)
                sp.dma_start(slots_y[bass.ds(s * P, P), :], l.y[:, :]).then_inc(l.y_out, 16)

            for n, l in enumerate(lane):
                load(l, n)
            with sp.Fori(0, TILES // 2 - 1) as i:
                for n, l in enumerate(lane):
                    sp.wait_ge(l.pe, 6 * i + 1)
                    sp.sem_inc(stored, 1)
                    load(l, 2 * i + (2 + n))
                for n, l in enumerate(lane):
                    store(l, 2 * i + n, i)
            last = TILES // 2 - 1
            for n, l in enumerate(lane):
                store(l, 2 * last + n, last)
            sp.wait_ge(final, 1)
            sp.dma_start(out.rearrange("b (q p) d -> p (b q) d", p=P), gathered[:, :, 0, :]).then_inc(zeroed, 16)
            sp.wait_ge(zeroed, 32)

        @block.gpsimd
        def _(pool):
            G = nc.gpsimd
            count = Tally(made)

            def did(ins):
                ins.then_inc(made, 1)
                count.n += 1
                pool.wait_ge(made, count.value())

            did(G.memset(zeros[:, :], 0.0))
            did(G.memset(ones[:, :], 1.0))
            did(G.affine_select(out=tri[:, :], in_=ones[:, :], compare_op=ALU.is_gt, fill=0.0, base=0,
                                pattern=[[1, P]], channel_multiplier=-1))
            did(G.iota(counting[:, :], pattern=[[1, TILES]], base=0, channel_multiplier=0))
            did(G.memset(neg_half[:, :], -0.5))
            did(G.memset(ones_ne[:, :], 1.0))
            pool.wait_ge(small, 48)
            for n, ins in enumerate((lambda: G.tensor_copy(bias_split[:, 0, :], bias_raw[:, :]),
                                     lambda: G.tensor_tensor(bias_raw[:, :], bias_raw[:, :], bias_split[:, 0, :], ALU.subtract),
                                     lambda: G.tensor_copy(bias_split[:, 1, :], bias_raw[:, :]),
                                     lambda: G.tensor_tensor(bias_split[:, 2, :], bias_raw[:, :], bias_split[:, 1, :], ALU.subtract))):
                ins().then_inc(bias_done, 1)
                pool.wait_ge(bias_done, n + 1)
            pool.wait_ge(zeroed, 16)
            pool.wait_ge(routed, 1)
            for t in range(NT):
                for c in range(2):
                    G.indirect_dma_start(out=slots_x[:, :], out_offset=bass.IndirectOffsetOnAxis(ap=slot[:, t, c:c + 1], axis=0),
                                         in_=x2[:, t, :], in_offset=None).then_inc(scattered, 16)
            for l in lane:
                pool.wait_ge(l.y_out, 16 * (TILES // 2 + 1))
            for t in range(NT):
                for c in range(2):
                    G.indirect_dma_start(out=gathered[:, t, c, :], out_offset=None, in_=slots_y[:, :],
                                         in_offset=bass.IndirectOffsetOnAxis(ap=slot[:, t, c:c + 1], axis=0)).then_inc(got, 16)
            pool.wait_ge(var_ready, 1)
            G.tensor_tensor(rstd[:, :], ve[:, :], neg_half[:, :], ALU.pow).then_inc(rstd_ready, 1)

        @block.tensor
        def _(pe):
            pe.wait_ge(made, MADE)
            for t in range(NT):
                for k in range(2):
                    last = nc.tensor.transpose(x_banks[t // 2][:, (2 * (t % 2) + k) * P:(2 * (t % 2) + k + 1) * P],
                                               x2[:, t, k * P:(k + 1) * P], ident[:, :])
                if t % 2:
                    last.then_inc(pe_r, 1)
            pe.wait_ge(chain, 4)
            pe.wait_ge(small, 48)
            for t in range(NT):
                for k in range(2):
                    last = nc.tensor.matmul(route[:, t * NE:(t + 1) * NE], x2T[:, 2 * t + k, :], wg[:, k, :],
                                            start=(k == 0), stop=(k == 1))
            last.then_inc(pe_r, 1)
            pe.wait_ge(hot_ready, 1)
            for t in range(NT):
                for before in range(t + 1):
                    nc.tensor.matmul(route[:, 128 + t * NE:128 + (t + 1) * NE], tri[:, :] if before == t else ones[:, :],
                                     both[:, before, :], start=(before == 0), stop=(before == t))
            for t in range(NT):
                last = nc.tensor.matmul(route[:, 256:256 + NE], ones[:, :], both[:, t, :], start=(t == 0), stop=(t == NT - 1))
            last.then_inc(pe_r, 1)
            pe.wait_ge(routed, 1)
            pe.wait_ge(bias_in, 48)
            for e in range(NE):
                pe.wait_ge(weights[e], 48)

            def transposes(l, src, n):
                for k in range(n):
                    last = nc.tensor.transpose(l.bt[:, k * P:(k + 1) * P], src[:, k * P:(k + 1) * P], ident[:, :])
                last.then_inc(l.pe, 1)

            def layer(l, bank, xT, k_tiles, n, e, at, bias_at):
                nc.tensor.matmul(bank[:, 0:n], ones[0:PARTS, :], bias[0:PARTS, bass.ds(e * BE + bias_at, n)], start=True, stop=False)
                for k in range(k_tiles):
                    last = nc.tensor.matmul(bank[:, 0:n], xT[:, k, :], w[:, bass.ds(e * WE + (at + k * n), n)],
                                            start=False, stop=(k == k_tiles - 1))
                last.then_inc(l.pe, 1)

            with pe.Fori(0, TILES // 2) as i:
                es = []
                for n, l in enumerate(lane):
                    es.append(pe.value_load(expert[0:1, bass.ds(2 * i + n, 1)], min_val=0, max_val=NE - 1))
                for l in lane:
                    pe.wait_ge(l.x_in, 16 * i + 16)
                    pe.wait_ge(l.dve, 4 * i + 3)
                    transposes(l, l.xt, 2)
                for l, e in zip(lane, es):
                    pe.wait_ge(l.dve, 4 * i + (4 + 1))
                    pe.wait_ge(l.act, 2 * i + 1)
                    layer(l, l.bh, l.xT, D // P, FH, e, 0, 0)
                for l in lane:
                    pe.wait_ge(l.act, 2 * i + 2)
                    transposes(l, l.h, 4)
                for l, e in zip(lane, es):
                    pe.wait_ge(l.dve, 4 * i + (4 + 2))
                    layer(l, l.bh, l.hT[0], FH // P, FH, e, 2 * FH, FH)
                for l in lane:
                    pe.wait_ge(l.act, 2 * i + 3)
                    transposes(l, l.h, 4)
                for l, e in zip(lane, es):
                    pe.wait_ge(l.dve, 4 * i + (4 + 3))
                    layer(l, l.by, l.hT[1], FH // P, D, e, 6 * FH, 2 * FH)

        @block.scalar
        def _(act):
            for l in lane:
                act.sem_inc(l.act, 1)
            act.wait_ge(away_ready, 1)
            nc.scalar.activation(expd[:, :, :], away[:, :, :], ACT.Exp).then_inc(exp_done, 1)
            with act.Fori(0, TILES // 2) as i:
                for layer in range(2):
                    for l in lane:
                        act.wait_ge(l.pe, 6 * i + (2 + 2 * layer))
                        nc.scalar.activation(l.h[:, :], l.bh[:, :], ACT.Gelu).then_inc(l.act, 1)

        @block.vector
        def _(dve):
            V = nc.vector
            ch = Tally(chain)

            def link(ins):
                ins.then_inc(chain, 1)
                ch.n += 1
                dve.wait_ge(chain, ch.value())

            for l in lane:
                dve.sem_inc(l.dve, 4)
                dve.sem_inc(l.y_out, 16)
            dve.wait_ge(made, MADE)
            for j in range(4):
                dve.wait_ge(pe_r, j + 1)
                V.tensor_copy(x2T[:, 4 * j:4 * j + 4, :].rearrange("p k q -> p (k q)"), x_banks[j][:, :]).then_inc(chain, 1)
                ch.n += 1
            link(V.tensor_copy(count_f[:, :], counting[:, :]))
            link(V.tensor_scalar(count_128[:, :], count_f[:, 0:NE], float(P), None, ALU.mult))
            dve.wait_ge(small, 48)
            dve.wait_ge(pe_r, 5)
            link(V.tensor_tensor(logits[:, :, :], route[:, 0:NT * NE].rearrange("p (t e) -> p t e", t=NT),
                                 bg[:, :].unsqueeze(1).to_broadcast([P, NT, NE]), ALU.add))
            for t in range(NT):
                ins = V.max(best[:, t, :], logits[:, t, :])
            link(ins)
            for t in range(NT):
                ins = V.max_index(best_at[:, t, :], best[:, t, :], logits[:, t, :])
            link(ins)
            V.tensor_tensor(away[:, :, :], best[:, :, :], best[:, :, 0:1].to_broadcast([P, NT, NE]), ALU.subtract).then_inc(away_ready, 1)
            link(V.tensor_copy(best_f[:, :, :], best_at[:, :, 0:2]))
            link(V.tensor_tensor(hot[:, :, :, :], count_f[:, 0:NE].unsqueeze(1).unsqueeze(1).to_broadcast([P, NT, 2, NE]),
                                 best_f[:, :, :].unsqueeze(3).to_broadcast([P, NT, 2, NE]), ALU.is_equal))
            V.tensor_tensor(both[:, :, :], hot[:, :, 0, :], hot[:, :, 1, :], ALU.add).then_inc(hot_ready, 1)
            dve.wait_ge(exp_done, 1)
            link(V.tensor_reduce(total[:, 0, :], expd[:, :, :], X, ALU.add))
            link(V.reciprocal(total[:, 1, :], total[:, 0, :]))
            link(V.tensor_tensor(gate[:, :, :], expd[:, :, 0:2], total[:, 1, :].unsqueeze(2).to_broadcast([P, NT, 2]), ALU.mult))
            dve.wait_ge(pe_r, 6)
            link(V.tensor_tensor(many[:, :, :], route[:, 256:256 + NE].unsqueeze(2).to_broadcast([P, NE, NE]),
                                 count_128[:, :].unsqueeze(1).to_broadcast([P, NE, NE]), ALU.is_gt))
            link(V.tensor_reduce(tiles_of[:, :], many[:, :, :], X, ALU.add))
            link(V.tensor_tensor_scan(end[:, :], ones_ne[:, :], tiles_of[:, :], 0.0, ALU.mult, ALU.add))
            link(V.tensor_tensor(first[:, :], end[:, :], tiles_of[:, :], ALU.subtract))
            link(V.tensor_scalar(tiles_of[:, :], first[:, :], float(P), None, ALU.mult))
            link(V.tensor_tensor(place[:, :, :], route[:, 128:128 + NT * NE].rearrange("p (t e) -> p t e", t=NT),
                                 tiles_of[:, :].unsqueeze(1).to_broadcast([P, NT, NE]), ALU.add))
            link(V.tensor_tensor(place_hot[:, :, :, :], hot[:, :, :, :],
                                 place[:, :, :].unsqueeze(2).to_broadcast([P, NT, 2, NE]), ALU.mult))
            link(V.tensor_reduce(slot_f[:, :, :], place_hot[:, :, :, :], X, ALU.add))
            link(V.tensor_copy(slot[:, :, :], slot_f[:, :, :]))
            link(V.tensor_tensor(past[:, :, :], count_f[:, :].unsqueeze(2).to_broadcast([P, TILES, NE]),
                                 end[:, :].unsqueeze(1).to_broadcast([P, TILES, NE]), ALU.is_ge))
            link(V.tensor_reduce(expert_f[:, 0, :], past[:, :, :], X, ALU.add))
            link(V.tensor_scalar(expert_f[:, 1, :], expert_f[:, 0, :], float(NE - 1), None, ALU.min))
            V.tensor_copy(expert[:, :], expert_f[:, 1, :]).then_inc(routed, 1)
            with dve.Fori(0, TILES // 2) as i:
                for step in range(3):
                    for l in lane:
                        dve.wait_ge(l.pe, 6 * i + (1 + 2 * step))
                        if step == 0:
                            ins = V.tensor_copy(l.xT[:, :, :].rearrange("p k q -> p (k q)"), l.bt[:, 0:D])
                        else:
                            ins = V.tensor_copy(l.hT[step - 1][:, :, :].rearrange("p k q -> p (k q)"), l.bt[:, :])
                        ins.then_inc(l.dve, 1)
                for l in lane:
                    dve.wait_ge(l.pe, 6 * i + 6)
                    dve.wait_ge(l.y_out, 16 * i + 16)
                    V.tensor_copy(l.y[:, :], l.by[:, 0:D]).then_inc(l.dve, 1)
            dve.wait_ge(got, 16 * 2 * NT)
            for c in range(2):
                for t in range(NT):
                    base = x2[:, t, :] if c == 0 else y[:, t, :]
                    ins = V.scalar_tensor_tensor(out=y[:, t, :], in0=gathered[:, t, c, :], scalar=gate[:, t, c:c + 1],
                                                 in1=base, op0=ALU.mult, op1=ALU.add)
                link(ins)
            for t in range(NT):
                ins = V.bn_stats(stats[:, t, :], y[:, t, :])
            link(ins)
            for t in range(NT):
                ins = V.bn_aggr(mv[:, t, :], stats[:, t, :])
            link(ins)
            V.tensor_scalar(ve[:, :], mv[:, :, 1], EPS, None, ALU.add).then_inc(var_ready, 1)
            dve.wait_ge(rstd_ready, 1)
            for t in range(NT):
                ins = V.tensor_scalar(gathered[:, t, 0, :], y[:, t, :], mv[:, t, 0:1], rstd[:, t:t + 1], ALU.subtract, ALU.mult)
            ins.then_inc(final, 1)



def program(nc, a, out):
    ca, cx = finish_shape(self_attention_shape()), finish_shape(cross_attention_shape())
    ca.chain_turn, cx.chain_turn = 4 * 4 + 4 + 3, 4 * 4 + 4 + 6 + 6 + 4
    scratch = {c.name: nc.dram_tensor(f"parts_{c.name}", [2, PARTS, P, S + c.T], BF16, kind="Internal").ap()
               for c in (ca, cx)}
    outer = ExitStack()
    with outer:
        x2, ident, ident_bf = (outer.enter_context(nc.sbuf_tensor(n, sh, dt)) for n, sh, dt in (
            ("x_in_out", [P, NT, D], F32), ("ident", [P, P], F32), ("ident_bf", [P, P], BF16)))
        attention_block(nc, a, ca, cx, scratch, x2, ident, ident_bf)
        experts_block(nc, a, out, x2, ident, ident_bf)


def attention_block(nc, a, ca, cx, scratch, x2, ident, ident_bf):
    ctx = ExitStack()
    with ctx:
        def sb(name, shape, dt=F32):
            return ctx.enter_context(nc.sbuf_tensor(name, shape, dt))

        def ps(name, w):
            return ctx.enter_context(nc.psum_tensor(name, [P, w], F32))

        mbank = [ps(f"m_bank{i}", 512) for i in range(M_RING)]
        stbank = [ps(f"st_bank{i}", 1024) for i in range(ST_RING)]
        obank = ps("o_bank", 512)

        loaded = ctx.enter_context(nc.semaphore("loaded"))
        made = ctx.enter_context(nc.semaphore("made"))
        sa, sx = attention_sems(ctx, nc, ca), attention_sems(ctx, nc, cx)

        x0 = x2
        x1 = sb("x1", [P, NT, D])
        common = dict(mbank=mbank, stbank=stbank, obank=obank, loaded=loaded, made=made, ident=ident, ident_bf=ident_bf)
        common.update(
            probs=[sb(f"probs{i}", [P, 1024]) for i in range(PROB_RING)],
            mparts=sb("max_parts", [P, 2 * UH, PARTS], BF16), nm=sb("neg_max", [P, 2, 2 * UH]),
            oT_unit=sb("oT_unit", [P, S]), rden=sb("rden", [P, 2, UH]), o_tm=sb("o_tokens", [P, 2, D]),
            oT=sb("oT", [P, 2, S]), y=sb("y", [P, 2, D]), y2=sb("y_biased", [P, 2, D]), stats=sb("stats", [P, 2, 6]),
            mv=sb("mean_var", [P, 2, 2]), ve=sb("var_eps", [P, 2]), rstd=sb("rstd", [P, 2]),
            neg_half=sb("neg_half", [P, 2]), qs=sb("quant_scale", [P, 3, 2]),
            qa=sb("quant_a", [P, 2, D]), qb=sb("quant_b", [P, 2, D]),
            cmask=sb("causal_mask", [P, 2, S]), junk=sb("masked_scores", [P, 2 * UH, S]),
            qst=[sb(f"q_stack{m}", [P, HH, S], BF16) for m in range(2)],
            )
        kst = [sb(f"k_stack{m}", [P, HH, SK], BF16) for m in range(2)]
        vaug = [sb(f"v_ones{m}", [P, len(cx.tiles), HH, VW]) for m in range(2)]
        f = sb("qk_rows", [P, S + SK])
        parts = sb("qk_parts", [P, PARTS, S + SK], BF16)
        parts_sa = sb("qk_parts_self", [P, PARTS, 2 * S], BF16)
        xT = sb("ctxT", [P, 2, SK])
        xTs = sb("xT", [P, 2, S])
        wts = {n: sb(n, [P, 2, D]) for n in ("w_q", "w_k", "w_v", "w_o", "xw_q", "xw_p", "xw_qq", "xw_pq",
                                             "xw_k", "xw_v")}
        bq, bk = sb("bq", [P, 2]), sb("bk", [P, 2])
        bv, bp = sb("bv", [P, D]), sb("bp", [P, D])

        ta = NS(**{**common, "mx": sb("row_max_self", [P, 2 * UH, 1]), "kst": kst, "vaug": vaug, "f": f[:, 0:2 * S],
                   "parts": parts_sa, "xT": xTs, "wq": wts["w_q"], "wk": wts["w_k"],
                   "wv": wts["w_v"], "wo": wts["w_o"], "x_in": x0, "x_out": x1})
        tx = NS(**{**common, "mx": sb("row_max", [P, 2 * UH, cx.NC]), "kst": kst, "vaug": vaug, "f": f,
                   "parts": parts, "xT": xT, "wq": wts["xw_q"], "wk": wts["xw_k"], "wv": wts["xw_v"],
                   "wo": wts["xw_p"], "wq_raw": wts["xw_q"], "wp_raw": wts["xw_p"], "wq_q": wts["xw_qq"],
                   "wp_q": wts["xw_pq"], "xq": sb("x_quant", [P, 2, D]), "oq": sb("o_quant", [P, 2, D]),
                   "xqT": sb("xqT", [P, 2, S]), "bq": bq, "bk": bk, "bv": bv, "bp": bp, "x_in": x1, "x_out": x2})
        rows = lambda w: w.rearrange("(k p) n -> p k n", p=P)
        loads = [(x0, a["x"].rearrange("b (q p) d -> p (b q) d", p=P)), (wts["w_q"], rows(a["w_q"])),
                 (wts["w_k"], rows(a["w_k"])), (wts["w_v"], rows(a["w_v"])), (wts["w_o"], rows(a["w_o"])),
                 (wts["xw_q"], rows(a["xw_q"])), (wts["xw_p"], rows(a["xw_p"])),
                 (wts["xw_k"], rows(a["xw_kvT"][:, 0:D])), (wts["xw_v"], rows(a["xw_kvT"][:, D:2 * D])),
                 (bq, a["bq"]), (bk, a["bkv"][:, 0:2]), (bv, a["bv"].partition_broadcast(P)), (bp, a["bp"].partition_broadcast(P))]
        ta.loaded_all = tx.loaded_all = 16 * len(loads)
        MADE = 8 + 3
        block = ctx.enter_context(nc.Block())

        @block.scalar
        def _(act):
            for dst, src in loads:
                act.dma_start(dst[:, :, :] if len(dst.shape) == 3 else dst[:, :], src).then_inc(loaded, 16)
            act.wait_ge(loaded, ta.loaded_all)
            act_attention(nc, act, ca, sa, ta)
            act_attention(nc, act, cx, sx, tx)

        @block.gpsimd
        def _(pool):
            G = nc.gpsimd
            count = Tally(made)

            def did(ins):
                ins.then_inc(made, 1)
                count.n += 1
                pool.wait_ge(made, count.value())

            did(G.memset(ident[:, :], 0.0))
            did(G.memset(ident_bf[:, :], 0.0))
            did(G.memset(common["cmask"][:, :, :], 0.0))
            did(G.memset(common["neg_half"][:, :], -0.5))
            for m in range(2):
                did(G.memset(kst[m][MROW:STACK, :, :], 1.0))
                did(G.memset(vaug[m][:, :, :, DH:VW], 1.0))
            for w in (ident, ident_bf):
                did(G.affine_select(out=w[:, :], in_=w[:, :], compare_op=ALU.not_equal, fill=1.0, base=0,
                                pattern=[[-1, P]], channel_multiplier=1))
            did(G.affine_select(out=common["cmask"][:, :, :], in_=common["cmask"][:, :, :], compare_op=ALU.is_ge, fill=MASK,
                            base=0, pattern=[[P, 2], [-1, S]], channel_multiplier=1))
            assert count.n == MADE
            pool_attention(nc, pool, ca, sa, ta)
            pool_attention(nc, pool, cx, sx, tx)

        @block.vector
        def _(dve):
            dve.wait_ge(made, MADE)
            dve.wait_ge(loaded, ta.loaded_all)
            dve_attention(nc, dve, ca, sa, ta)
            dve_attention(nc, dve, cx, sx, tx)

        @block.tensor
        def _(pe):
            pe.wait_ge(made, MADE)
            pe.wait_ge(loaded, ta.loaded_all)
            nc.tensor.matmul(obank[:, 0:S], ident[:, :], common["cmask"][:, 0, :], start=True, stop=True)
            pe_attention(nc, pe, ca, sa, ta)
            pe_attention(nc, pe, cx, sx, tx)

        @block.sync
        def _(sp):
            sp_attention(nc, sp, ca, sa, ta, a["xT"], scratch["sa"])
            sp.wait_ge(sa.act_done, ST_RING + B * ca.st_turn)
            sp_attention(nc, sp, cx, sx, tx, a["ctxT"], scratch["xa"])


def kernel(**inputs):
    import numpy as np
    import concourse.bacc as bacc
    from concourse import mybir as mb
    from concourse.bass_utils import run_bass_kernel_spmd

    g = {k: np.asarray(v) for k, v in inputs.items()}
    arrays = {
        "x": g["x"], "xT": g["x"].transpose(0, 2, 1), "ctxT": g["ctx_2048"].transpose(0, 2, 1),
        "w_q": g["L0_attn_q_wei"], "w_k": g["L0_attn_k_wei"], "w_v": g["L0_attn_v_wei"], "w_o": g["L0_attn_out_wei"],
        "xw_q": g["L0_xattn_wq"], "xw_p": g["L0_xattn_wp"], "xw_kvT": g["L0_xattn_wkv"].T,
        "bq": g["L0_xattn_bq"].reshape(2, 128).T, "bkv": g["L0_xattn_bkv"].reshape(4, 128).T,
        "W1": g["L0_ffn_W1"], "W2": g["L0_ffn_W2"], "W3": g["L0_ffn_W3"], "wg": g["L0_ffn_Wg"], "bg": g["L0_ffn_bg"],
        "bias": np.concatenate([g["L0_ffn_b1"], g["L0_ffn_b2"], g["L0_ffn_b3"]], axis=1),
        "bv": g["L0_xattn_bkv"][256:], "bp": g["L0_xattn_bp"],
    }
    arrays = {k: np.ascontiguousarray(v) for k, v in arrays.items()}
    nc = bacc.Bacc("TRN2", target_bir_lowering=False, num_devices=1)
    aps = {k: nc.dram_tensor("in_" + k, v.shape, mb.dt.from_np(v.dtype), kind="ExternalInput").ap() for k, v in arrays.items()}
    out = nc.dram_tensor("out_0", (4, 256, 256), mb.dt.float32, kind="ExternalOutput").ap()
    program(nc, aps, out)
    r = run_bass_kernel_spmd(nc, [{"in_" + k: v for k, v in arrays.items()}], core_ids=[0])
    return r.results[0]["out_0"]
```

```python
import concourse.bass as bass
from concourse import mybir
from contextlib import ExitStack

F32 = mybir.dt.float32
BF16 = mybir.dt.bfloat16
I32 = mybir.dt.int32
U32 = mybir.dt.uint32
ALU = mybir.AluOpType
ACT = mybir.ActivationFunctionType
X = mybir.AxisListType.X

B, S, D, H, DH = 4, 256, 256, 16, 16
SK = 1601
P = 128
NT = B * S // P
HH = H // 2
UH = 4
PARTS = 3
Q_PARTS = (0, 1, 2, 0, 1, 0)
K_PARTS = (0, 0, 0, 1, 1, 2)
NPROD = len(Q_PARTS)
MROW = NPROD * DH
STACK = MROW + PARTS
VW = DH + 1
NE, FH = 8, 512
WE = (D * FH + FH * FH + FH * D) // P
BE = FH + FH + D
TILES = 2 * B * S // P + NE
MASK = -66504.0
EPS = 1e-5
ROUND = 12582912.0
M_RING, ST_RING, PROB_RING = 3, 2, 4
SPLIT_AT = 2
PV_LAG = 1


def NS(**named):
    return type("Named", (), named)


class Tally:

    def __init__(self, sem, credit=0):
        self.sem, self.credit, self.n = sem, credit, 0
        self.turn = self.per_turn = 0
        self.marks = {}

    def enter(self, turn, per_turn):
        self.turn, self.per_turn, self.start = turn, per_turn, self.n

    def leave(self, turns):
        assert self.n == self.start + self.per_turn, (self.sem, self.n - self.start, self.per_turn)
        more = (turns - 1) * self.per_turn
        self.n += more
        self.marks = {k: v + more for k, v in self.marks.items()}
        self.turn = 0

    def value(self, more=0):
        return self.turn * self.per_turn + (self.n + more)

    def done(self, more=0):
        return self.turn * self.per_turn + (self.n + more + self.credit)

    def mark(self, what):
        self.marks[what] = self.n

    def marked(self, what):
        return self.turn * self.per_turn + (self.marks[what] + self.credit)


def self_attention_shape():
    c = NS(name="sa", cross=False, T=S, tiles=[P] * (S // P), chunks=[(0, S)])
    c.groups = [[0, 1]]
    return c


def cross_attention_shape():
    c = NS(name="xa", cross=True, T=SK, tiles=[P] * (SK // P) + [SK % P])
    c.chunks = [(i * 400 + min(i, 1), 401 if i == 0 else 400) for i in range(4)]
    assert c.chunks[-1][0] + c.chunks[-1][1] == SK
    c.groups = [list(range(i, min(i + 4, len(c.tiles)))) for i in range(0, len(c.tiles), 4)]
    return c


def finish_shape(c):
    c.NC = len(c.chunks)
    c.max_jobs = 2 * UH * c.NC
    c.vjobs = -(-len(c.tiles) // 4)
    c.kjobs = 2 if c.cross else 0
    c.st_unit = UH * len(c.groups)
    jobs = (2 + c.cross) + 2 * c.vjobs + 4 * (3 + c.max_jobs) + 2
    c.pad = -jobs % M_RING
    st_turn, pv_turn = 2 * c.kjobs + 4 * c.st_unit, 4 * c.st_unit
    assert st_turn % ST_RING == 0 and pv_turn % PROB_RING == 0
    c.chain_turn = 4 * 4 + 4 + (6 + 6 + 4 if c.cross else 2 * 2 + 3)
    c.turn = dict(m=jobs + c.pad, st=st_turn, o=4, pv=pv_turn, rows=4, chain=c.chain_turn)
    return c


def plan(c, after, pending, output):
    ns = c.st_unit
    jobs = [[] for _ in range(ns)]
    if after:
        slots = ns - 2 - ns // 16
        for i in range(after.max_jobs):
            jobs[i * slots // after.max_jobs].append("max")
    if pending:
        jobs[max(1, len(c.groups) - 1)].append("o")
    if output:
        jobs[ns // 2 + ns // 4 - ns // 5 + 1 if ns > 4 else 2].append("output_transposes")
    if after:
        jobs[ns - 1].append("rows")
    if output:
        jobs[ns - 1].append("output_product")
    return jobs


def attention_sems(ctx, nc, c):
    names = ("w_ready xq_ready oq_ready q_taken rest_ready middle_ready parts_ready scratch_written stack0_loaded stack1_loaded "
             "x_loaded x_used var_ready rstd_ready")
    return NS(**{n: ctx.enter_context(nc.semaphore(f"{c.name}_{n}")) for n in names.split()})


def ring_sems(ctx, nc):
    names = "m_full m_free st_full act_done o_free pv_done rows_ready masked dve_chain turnstile"
    return NS(**{n: ctx.enter_context(nc.semaphore(n)) for n in names.split()})


def run_layers(eng, tallies, la, lx, prologue, turn, final):
    prologue(la)
    for l in (la, lx):
        with eng.Fori(0, B - 1) as b:
            for name, x in tallies.items():
                x.enter(b, l.c.turn[name])
            turn(l, b, l, b + 1)
        for x in tallies.values():
            x.leave(B - 1)
        if l is la:
            turn(la, B - 1, lx, 0)
    final(lx, B - 1)



def pe_attention(nc, pe, r, la, lx):
    mt = Tally(r.m_free, M_RING)
    st = Tally(r.act_done, ST_RING)
    ot = Tally(r.o_free, 1)
    pt = Tally(r.pv_done, PROB_RING)
    mp = Tally(r.rows_ready)
    t = la.t
    late = []

    def m_bank():
        pe.wait_ge(mt.sem, mt.value(1))
        return t.mbank[mt.n % M_RING]

    def m_done(last, n=1):
        last.then_inc(r.m_full, n)
        mt.n += n

    def m_drained():
        pe.wait_ge(mt.sem, mt.done())

    def transposes(src, ready=None):
        bank = m_bank()
        if ready is not None:
            pe.wait_ge(*ready)
        for tt in range(2):
            for k in range(2):
                last = nc.tensor.transpose(bank[:, (2 * k + tt) * P:(2 * k + tt + 1) * P],
                                           src[:, tt, k * P:(k + 1) * P], t.ident[:, :])
        m_done(last)

    def project_qk(l, b, m):
        c, t = l.c, l.t
        pe.wait_ge(l.s.x_loaded, b * 16 + 16)
        ms = slice(m * P, (m + 1) * P)
        for pair in ((0, 1), (2, 3))[:c.kjobs]:
            pe.wait_ge(st.sem, st.value(1))
            bank = t.stbank[st.n % ST_RING]
            for i, ch in enumerate(pair):
                a, w = c.chunks[ch]
                for k in range(2):
                    last = nc.tensor.matmul(bank[:, i * 512:i * 512 + w], t.wk[:, k, ms], t.xT[:, k, a:a + w],
                                            start=(k == 0), stop=(k == 1))
            last.then_inc(r.st_full, 1)
            st.n += 1
        if c.cross and m == 0:
            transposes(t.xq, (l.s.xq_ready, b + 1))
            m_drained()
        bank = m_bank()
        for k in range(2):
            rhs = t.xqT[:, k, :] if c.cross else t.xT[:, k, :]
            last = nc.tensor.matmul(bank[:, 0:S], t.wq[:, k, ms], rhs, start=(k == 0), stop=(k == 1))
        if not c.cross:
            for k in range(2):
                last = nc.tensor.matmul(bank[:, S:2 * S], t.wk[:, k, ms], t.xT[:, k, :], start=(k == 0), stop=(k == 1))
        m_done(last)

    def project_v(l, b, m):
        c, t = l.c, l.t
        for v in range(c.vjobs):
            bank = m_bank()
            for i, kt in enumerate(range(4 * v, min(4 * v + 4, len(c.tiles)))):
                n = c.tiles[kt]
                for k in range(2):
                    last = nc.tensor.matmul(bank[0:n, i * P:(i + 1) * P], t.xT[:, k, kt * P:kt * P + n],
                                            t.wv[:, k, m * P:(m + 1) * P], start=(k == 0), stop=(k == 1))
            m_done(last)

    def between_steps(project, l, b, m):
        if l.c.cross:
            flush()
        project(l, b, m)
        flush()

    def stack_loaded(l, b, m):
        pe.wait_ge((l.s.stack0_loaded, l.s.stack1_loaded)[m], b * 192 + 192)

    def max_jobs(l, unit):
        m, g = unit
        for j in range(UH):
            h = UH * g + j
            for qt in range(2):
                for a, w in l.c.chunks:
                    bank = m_bank()
                    m_done(nc.tensor.matmul(bank[:, 0:w], t.qst[m][0:MROW, h, qt * P:(qt + 1) * P],
                                            t.kst[m][0:MROW, h, a:a + w], start=True, stop=True))
                    yield

    def rows_of_max():
        pe.wait_ge(mp.sem, mp.value(1))
        mp.n += 1
        for jb in range(2):
            bank = m_bank()
            for u in range(4):
                last = nc.tensor.matmul(bank[MROW:STACK, u * P:(u + 1) * P], t.mparts[:, 4 * jb + u, :], t.ident_bf[:, :],
                                        start=True, stop=True)
            m_done(last)
        mt.mark("rows")

    def pv(l, unit, j, grp, n_st, first, final):
        m, g = unit
        h = UH * g + j
        if first:
            pe.wait_ge(ot.sem, ot.value(1))
        if l.c.cross:
            pe.wait_ge(r.act_done, st.turn * st.per_turn + (n_st + 1 + ST_RING))
        else:
            pe.wait_ge(r.masked, pt.value(1))
        slot = t.probs[pt.n % PROB_RING]
        tiles = l.c.tiles
        for i, kt in enumerate(grp):
            n = tiles[kt]
            last = nc.tensor.matmul(t.obank[32 * j:32 * j + VW, 0:S], t.vaug[m][0:n, kt, h, :],
                                    slot[0:n, i * S:(i + 1) * S], start=(kt == 0), stop=(kt == len(tiles) - 1))
        last.then_inc(r.pv_done, 1)
        pt.n += 1
        if final:
            ot.n += 1

    def flush():
        while late:
            pv(*late.pop(0))

    def o_transposes():
        bank = m_bank()
        pe.wait_ge(ot.sem, ot.done())
        for qt in range(2):
            last = nc.tensor.transpose(bank[:, qt * P:(qt + 1) * P], t.oT_unit[:, qt * P:(qt + 1) * P], t.ident[:, :])
        m_done(last)

    def output_transposes(l, b):
        if l.c.cross:
            transposes(l.t.oq, (l.s.oq_ready, b + 1))
        else:
            pe.wait_ge(mt.sem, mt.marked("o"))
            transposes(l.t.o_tm)
        mt.mark("oT")

    def output_product(l):
        pe.wait_ge(mt.sem, mt.marked("oT"))
        bank = m_bank()
        for tt in range(2):
            for k in range(2):
                last = nc.tensor.matmul(bank[:, tt * D:(tt + 1) * D], t.oT[:, k, tt * P:(tt + 1) * P], l.t.wo[:, k, :],
                                        start=(k == 0), stop=(k == 1))
        m_done(last, 1 + l.c.pad)

    def step(l, unit, after, pending, output=None):
        c = l.c
        m, g = unit
        more = max_jobs(*after) if after else iter(())
        pe.wait_ge(mt.sem, mt.marked("rows"))
        i = 0
        jobs = plan(c, after and after[0].c, pending, output)
        for j in range(UH):
            h = UH * g + j
            for gi, grp in enumerate(c.groups):
                pe.wait_ge(st.sem, st.value(1))
                bank = t.stbank[st.n % ST_RING]
                for k, kt in enumerate(grp):
                    n = c.tiles[kt]
                    last = nc.tensor.matmul(bank[0:n, k * S:(k + 1) * S], t.kst[m][0:STACK, h, kt * P:kt * P + n],
                                            t.qst[m][0:STACK, h, :], start=True, stop=True)
                last.then_inc(r.st_full, 1)
                late.append((l, unit, j, grp, st.n, j == 0 and gi == 0, i == c.st_unit - 1))
                st.n += 1
                for job in jobs[i]:
                    if job == "max":
                        next(more)
                    elif job == "o":
                        o_transposes()
                        mt.mark("o")
                    elif job == "output_transposes":
                        output_transposes(*output)
                    elif job == "rows":
                        rows_of_max()
                    else:
                        output_product(output[0])
                if len(late) > PV_LAG:
                    pv(*late.pop(0))
                i += 1

    def turn(l, b, ln, bn):
        between_steps(project_qk, ln, bn, 0)
        stack_loaded(l, b, 1)
        step(l, (0, 1), (l, (1, 0)), True)
        between_steps(project_v, ln, bn, 0)
        step(l, (1, 0), (l, (1, 1)), True)
        between_steps(project_qk, ln, bn, 1)
        stack_loaded(ln, bn, 0)
        step(l, (1, 1), (ln, (0, 0)), True)
        between_steps(project_v, ln, bn, 1)
        step(ln, (0, 0), (ln, (0, 1)), True, (l, b))
        flush()

    def prologue(l):
        project_qk(l, 0, 0)
        project_v(l, 0, 0)
        project_qk(l, 0, 1)
        pe.wait_ge(t.made, t.made_all)
        stack_loaded(l, 0, 0)
        for _ in max_jobs(l, (0, 0)):
            pass
        project_v(l, 0, 1)
        rows_of_max()
        step(l, (0, 0), (l, (0, 1)), False)
        pe.wait_ge(t.loaded_cross, t.cross_loads)
        pe.wait_ge(t.made_cross, 2)
        flush()
        transposes(lx.t.wq_q, (lx.s.w_ready, 1))
        transposes(lx.t.wp_q, (lx.s.w_ready, 2))

    def final(l, b):
        stack_loaded(l, b, 1)
        step(l, (0, 1), (l, (1, 0)), True)
        flush()
        step(l, (1, 0), (l, (1, 1)), True)
        flush()
        step(l, (1, 1), None, True)
        flush()
        o_transposes()
        output_transposes(l, b)
        output_product(l)

    pe.sem_inc(r.pv_done, PROB_RING)
    run_layers(pe, dict(m=mt, st=st, o=ot, pv=pt, rows=mp), la, lx, prologue, turn, final)



def dve_attention(nc, dve, r, la, lx):
    V = nc.vector
    mt = Tally(r.m_full)
    ot = Tally(r.pv_done, PROB_RING)
    ch = Tally(r.dve_chain)
    t = la.t

    def link(ins, plain=False):
        ins.then_inc(r.dve_chain, 1)
        ch.n += 1
        dve.wait_ge(ch.sem, ch.value())
        if plain:
            dve.sem_inc(r.turnstile, 1)

    def job(plain=False):
        dve.wait_ge(mt.sem, mt.value(1))
        if plain:
            dve.sem_inc(r.turnstile, 1)
        return t.mbank[mt.n % M_RING]

    def free(ins, n=1):
        ins.then_inc(r.m_free, n)
        mt.n += n

    def settled():
        dve.wait_ge(r.m_free, mt.value() + M_RING)

    def quantise(src, dst, ready):
        for _ in quantise_steps(src, dst, ready):
            pass

    def quantise_steps(src, dst, ready):
        t = lx.t
        link(V.tensor_reduce(t.qs[:, 0, :], src, X, ALU.max, apply_absolute_value=True))
        yield
        link(V.tensor_scalar(t.qs[:, 1, :], t.qs[:, 0, :], 1.0 / 127.0, 1e-8, ALU.mult, ALU.max))
        yield
        link(V.reciprocal(t.qs[:, 2, :], t.qs[:, 1, :]))
        yield
        scale, inverse = (t.qs[:, i, :].unsqueeze(2).to_broadcast([P, 2, D]) for i in (1, 2))
        link(V.tensor_tensor(t.qa[:, :, :], src, inverse, ALU.mult))
        yield
        link(V.tensor_scalar(t.qb[:, :, :], t.qa[:, :, :], ROUND, -ROUND, ALU.add, ALU.add))
        yield
        link(V.tensor_scalar(t.qa[:, :, :], t.qb[:, :, :], 127.0, -127.0, ALU.min, ALU.max))
        yield
        V.tensor_tensor(dst, t.qa[:, :, :], scale, ALU.mult).then_inc(ready, 1)

    def take_transposed(dst):
        bank = job()
        free(V.tensor_copy(dst.rearrange("p k t -> p (k t)"), bank[:, 0:2 * D]))

    def take_qk(l, b, m):
        s, t = l.s, l.t
        again = not (isinstance(b, int) and b == 0 and m == 0)
        if l.c.cross:
            if m == 0:
                if again:
                    dve.wait_ge(s.xq_ready, b)
                quantise(t.x_in[:, bass.ds(2 * b, 2), :], t.xq[:, :, :], s.xq_ready)
                take_transposed(t.xqT)
            bank = job()
            if again:
                dve.wait_ge(s.scratch_written, 32 * b + 16 * m)
            V.tensor_scalar(t.parts[:, 0, 0:S], bank[:, 0:S], t.bq[:, m:m + 1], None, ALU.add)
            free(V.tensor_scalar(t.f[:, 0:S], bank[:, 0:S], t.bq[:, m:m + 1], None, ALU.add))
            settled()
            dve.sem_inc(s.q_taken, 1)
        else:
            bank = job()
            if again:
                dve.wait_ge(s.scratch_written, 32 * b + 16 * m)
            link(V.tensor_copy(t.parts[:, 0, :], bank[:, :]))
            free(V.tensor_tensor(t.f[:, :], bank[:, :], t.parts[:, 0, :], ALU.subtract))
            settled()
            link(V.tensor_copy(t.parts[:, 1, :], t.f[:, :]))
            V.tensor_tensor(t.parts[:, 2, :], t.f[:, :], t.parts[:, 1, :], ALU.subtract).then_inc(s.parts_ready, 1)

    def take_v(l, b, m):
        c, t = l.c, l.t
        for v in range(c.vjobs):
            tiles = c.tiles[4 * v:4 * v + 4]
            n, k = tiles[0], len(tiles)
            bank = job()
            src = bank[0:n, 0:k * P].rearrange("p (k h d) -> p k h d", k=k, h=HH)
            dst = t.vaug[m][0:n, 4 * v:4 * v + k, :, 0:DH]
            if c.cross:
                for i in range(k):
                    bias = t.bv[0:n, m * P:(m + 1) * P].rearrange("p (h d) -> p h d", h=HH)
                    ins = V.tensor_tensor(dst[:, i], src[:, i], bias, ALU.add)
                free(ins)
            else:
                free(V.tensor_copy(dst, src))
        if m == 1:
            settled()
            dve.sem_inc(l.s.x_used, 1)

    def max_jobs(l, unit):
        t = l.t
        settled()
        for u in range(2 * UH):
            for i, (a, w) in enumerate(l.c.chunks):
                bank = job(plain=not l.c.cross)
                if l.c.cross:
                    free(V.reduce_max(t.mx[:, u, i:i + 1], bank[:, 0:w], X))
                else:
                    free(V.tensor_tensor_reduce(out=t.junk[:, u, :], in0=bank[:, 0:S], in1=t.cmask[:, u % 2, :],
                                                scale=1.0, scalar=-3.0e38, op0=ALU.add, op1=ALU.max,
                                                accum_out=t.mx[:, u, i:i + 1]))
                if u < 2 * UH - 1 or i < l.c.NC - 1:
                    yield
        settled()
        link(V.tensor_reduce(t.nm[:, 0, :], t.mx[:, :, :], X, ALU.max, negate=True))
        link(V.tensor_copy(t.mparts[:, :, 0], t.nm[:, 0, :]))
        link(V.tensor_tensor(t.nm[:, 1, :], t.nm[:, 0, :], t.mparts[:, :, 0], ALU.subtract))
        link(V.tensor_copy(t.mparts[:, :, 1], t.nm[:, 1, :]))
        V.tensor_tensor(t.mparts[:, :, 2], t.nm[:, 1, :], t.mparts[:, :, 1], ALU.subtract).then_inc(r.rows_ready, 1)
        yield

    def rows_of_max(unit):
        m, g = unit
        for jb in range(2):
            bank = job()
            h = UH * g + 2 * jb
            free(V.tensor_copy(t.qst[m][MROW:STACK, h:h + 2, :],
                               bank[MROW:STACK, 0:2 * S].rearrange("p (h q) -> p h q", h=2)))

    def copy_o(l):
        ot.n += l.c.st_unit
        dve.wait_ge(ot.sem, ot.done())
        V.tensor_copy(t.oT_unit[:, :], t.obank[:, 0:S]).then_inc(r.o_free, 1)

    def take_o(unit):
        m, g = unit
        bank = job()
        v = bank[:, 0:2 * P].rearrange("p (q j w) -> p q j w", q=2, j=UH)
        settled()
        link(V.reciprocal(t.rden[:, :, :], v[:, :, :, DH]))
        a = (m * HH + g * UH) * DH
        dst = t.o_tm[:, :, a:a + UH * DH].rearrange("p q (j d) -> p q j d", j=UH)
        free(V.tensor_tensor(dst, v[:, :, :, 0:DH], t.rden[:, :, :].unsqueeze(3).to_broadcast([P, 2, UH, DH]), ALU.mult))

    def step(l, unit, after, pending, output=None):
        more = max_jobs(*after) if after else iter(())
        quant = iter(())
        for i, jobs in enumerate(plan(l.c, after and after[0].c, pending, output)):
            for n, job_name in enumerate(jobs):
                if job_name == "max":
                    next(more)
                    if n % 2:
                        next(quant, None)
                elif job_name == "o":
                    take_o(pending)
                    if output and output[0].c.cross:
                        settled()
                        quant = quantise_steps(t.o_tm[:, :, :], lx.t.oq[:, :, :], lx.s.oq_ready)
                elif job_name == "output_transposes":
                    for _ in quant:
                        pass
                    take_transposed(t.oT)
                elif job_name == "rows":
                    rows_of_max(after[1])
        copy_o(l)
        if output:
            take_output(*output)

    def take_output(l, b):
        s, t = l.s, l.t
        bank = job()
        out = bank[:, 0:2 * D].rearrange("p (q d) -> p q d", q=2)
        free(V.tensor_tensor(t.y[:, :, :], out, t.x_in[:, bass.ds(2 * b, 2), :], ALU.add), 1 + l.c.pad)
        settled()
        y = t.y
        if l.c.cross:
            link(V.tensor_tensor(t.y2[:, :, :], t.y[:, :, :], t.bp[:, :].unsqueeze(1).to_broadcast([P, 2, D]), ALU.add))
            y = t.y2
        for q in range(2):
            ins = V.bn_stats(t.stats[:, q, :], y[:, q, :])
        link(ins, plain=True)
        for q in range(2):
            ins = V.bn_aggr(t.mv[:, q, :], t.stats[:, q, :])
        link(ins)
        V.tensor_scalar(t.ve[:, :], t.mv[:, :, 1], EPS, None, ALU.add).then_inc(s.var_ready, 1)
        dve.wait_ge(s.rstd_ready, b + 1)
        for q in range(2):
            ins = V.tensor_scalar(t.x_out[:, 2 * b + q, :], y[:, q, :], t.mv[:, q, 0:1], t.rstd[:, q:q + 1],
                                  ALU.subtract, ALU.mult)
        link(ins)

    def turn(l, b, ln, bn):
        take_qk(ln, bn, 0)
        step(l, (0, 1), (l, (1, 0)), (0, 0))
        take_v(ln, bn, 0)
        step(l, (1, 0), (l, (1, 1)), (0, 1))
        take_qk(ln, bn, 1)
        step(l, (1, 1), (ln, (0, 0)), (1, 0))
        take_v(ln, bn, 1)
        step(ln, (0, 0), (ln, (0, 1)), (1, 1), (l, b))

    def prologue(l):
        take_qk(l, 0, 0)
        take_v(l, 0, 0)
        take_qk(l, 0, 1)
        for _ in max_jobs(l, (0, 0)):
            pass
        take_v(l, 0, 1)
        rows_of_max((0, 0))
        step(l, (0, 0), (l, (0, 1)), None)
        dve.wait_ge(t.loaded_cross, t.cross_loads)
        quantise(lx.t.wq_raw[:, :, :], lx.t.wq_q[:, :, :], lx.s.w_ready)
        quantise(lx.t.wp_raw[:, :, :], lx.t.wp_q[:, :, :], lx.s.w_ready)
        take_transposed(lx.t.wq)
        take_transposed(lx.t.wo)

    def final(l, b):
        step(l, (0, 1), (l, (1, 0)), (0, 0))
        step(l, (1, 0), (l, (1, 1)), (0, 1))
        step(l, (1, 1), None, (1, 0))
        take_o((1, 1))
        settled()
        quantise(t.o_tm[:, :, :], l.t.oq[:, :, :], l.s.oq_ready)
        take_transposed(t.oT)
        take_output(l, b)

    dve.sem_inc(r.m_free, M_RING)
    dve.sem_inc(r.o_free, 1)
    run_layers(dve, dict(m=mt, pv=ot, chain=ch), la, lx, prologue, turn, final)



def act_attention(nc, act, r, la, lx):
    st = Tally(r.st_full)
    pt = Tally(r.pv_done, PROB_RING)

    def take_k(l, b, m):
        c, t = l.c, l.t
        for pair in ((0, 1), (2, 3))[:c.kjobs]:
            act.wait_ge(st.sem, st.value(1))
            if not (isinstance(b, int) and b == 0 and m == 0):
                act.wait_ge(l.s.scratch_written, 32 * b + 16 * m)
            bank = t.stbank[st.n % ST_RING]
            for i, chunk in enumerate(pair):
                a, w = c.chunks[chunk]
                for dst in (t.f, t.parts[:, 0, :]):
                    last = nc.scalar.activation(dst[:, S + a:S + a + w], bank[:, i * 512:i * 512 + w], ACT.Identity,
                                                bias=t.bk[:, m:m + 1])
            last.then_inc(r.act_done, 1)
            st.n += 1

    def middle_parts(l, b, m):
        if l.c.cross:
            act.wait_ge(l.s.rest_ready, 2 * b + (m + 1))
            nc.scalar.activation(l.t.parts[:, 1, :], l.t.f[:, :], ACT.Identity).then_inc(l.s.middle_ready, 1)

    def step(l, split=None):
        c, t = l.c, l.t
        for i, (j, grp) in enumerate((j, grp) for j in range(UH) for grp in c.groups):
                act.wait_ge(st.sem, st.value(1))
                act.wait_ge(pt.sem, pt.value(1))
                n = c.tiles[grp[0]]
                w = len(grp) * S
                nc.scalar.activation(t.probs[pt.n % PROB_RING][0:n, 0:w], t.stbank[st.n % ST_RING][0:n, 0:w],
                                     ACT.Exp, scale=float(DH) ** -0.5).then_inc(r.act_done, 1)
                st.n += 1
                pt.n += 1
                if split and i == SPLIT_AT:
                    middle_parts(*split)

    def turn(l, b, ln, bn):
        take_k(ln, bn, 0)
        step(l, (ln, bn, 0))
        step(l)
        take_k(ln, bn, 1)
        step(l, (ln, bn, 1))
        step(ln)

    def prologue(l):
        step(l)
        act.wait_ge(l.t.loaded_cross, l.t.cross_loads)

    def final(l, b):
        for _ in range(3):
            step(l)

    act.sem_inc(r.act_done, ST_RING)
    run_layers(act, dict(st=st, pv=pt), la, lx, prologue, turn, final)



def pool_attention(nc, pool, r, la, lx):
    G = nc.gpsimd
    st = Tally(r.act_done, ST_RING)
    pt = Tally(None)

    def split(l, b, m):
        if not l.c.cross:
            return
        s, t = l.s, l.t
        pool.wait_ge(s.q_taken, 2 * b + (m + 1))
        st.n += l.c.kjobs
        pool.wait_ge(st.sem, st.done())
        pool.sem_inc(r.turnstile, 1)
        G.tensor_tensor(t.f[:, :], t.f[:, :], t.parts[:, 0, :], ALU.subtract).then_inc(s.rest_ready, 1)

    def last_parts(l, b, m):
        if l.c.cross:
            s, t = l.s, l.t
            pool.wait_ge(s.middle_ready, 2 * b + (m + 1))
            pool.sem_inc(r.turnstile, 1)
            G.tensor_tensor(t.parts[:, 2, :], t.f[:, :], t.parts[:, 1, :], ALU.subtract).then_inc(s.parts_ready, 1)

    def step(l, split=None):
        t = l.t
        for i in range(l.c.st_unit):
            st.n += 1
            if not l.c.cross:
                pool.wait_ge(st.sem, st.done())
                pool.sem_inc(r.turnstile, 1)
                slot = t.probs[pt.n % PROB_RING][:, 0:2 * S].rearrange("p (k q) -> p k q", k=2)
                G.affine_select(out=slot, in_=slot, compare_op=ALU.is_ge, fill=0.0, base=0,
                                pattern=[[-P, 2], [1, S]], channel_multiplier=-1).then_inc(r.masked, 1)
            pt.n += 1
            if split and i == SPLIT_AT:
                last_parts(*split)

    def rstd(l, b):
        t = l.t
        pool.wait_ge(l.s.var_ready, b + 1)
        G.tensor_tensor(t.rstd[:, :], t.ve[:, :], t.neg_half[:, :], ALU.pow).then_inc(l.s.rstd_ready, 1)

    def turn(l, b, ln, bn):
        split(ln, bn, 0)
        step(l, (ln, bn, 0))
        step(l)
        split(ln, bn, 1)
        step(l, (ln, bn, 1))
        step(ln)
        rstd(l, b)

    def final(l, b):
        for _ in range(3):
            step(l)
        rstd(l, b)

    run_layers(pool, dict(st=st, pv=pt), la, lx, step, turn, final)



def sp_attention(nc, sp, r, la, lx):
    units = Tally(r.o_free, 1)

    def load_input(l, b):
        sp.dma_start(l.t.xT[:, :, :], l.x_dram[b, :, :].rearrange("(k p) t -> p k t", p=P)).then_inc(l.s.x_loaded, 16)

    def stacks(l, b, m, units_done):
        c, s, t, scratch = l.c, l.s, l.t, l.scratch
        sp.wait_ge(s.parts_ready, 2 * b + (m + 1))
        sp.sem_inc(r.turnstile, 1)
        sems = (s.stack0_loaded, s.stack1_loaded)
        if not (isinstance(b, int) and b == 0):
            sp.wait_ge(sems[m], 192 * b)
        sp.dma_start(scratch[m, :, :, :].rearrange("s f t -> f s t"), t.parts[:, :, :]).then_inc(s.scratch_written, 16)
        sp.wait_ge(s.scratch_written, 32 * b + (16 * m + 16))
        sp.sem_inc(r.turnstile, 1)
        if units_done is not None:
            sp.wait_ge(r.o_free, units_done)
        for i in range(NPROD):
            rows = slice(i * DH, (i + 1) * DH)
            sp.dma_start(t.kst[m][rows, :, 0:c.T], scratch[m, K_PARTS[i], :, S:].rearrange("(j d) t -> d j t", d=DH))\
                .then_inc(sems[m], 16)
            sp.dma_start(t.qst[m][rows, :, :], scratch[m, Q_PARTS[i], :, 0:S].rearrange("(j d) t -> d j t", d=DH))\
                .then_inc(sems[m], 16)

    def turn(l, b, ln, bn):
        if ln is l:
            sp.wait_ge(l.s.x_used, b + 1)
            sp.sem_inc(r.turnstile, 1)
            load_input(ln, bn)
        stacks(ln, bn, 0, units.done(2))
        stacks(ln, bn, 1, units.done(4))
        units.n += 4

    def prologue(l):
        for m in range(2):
            stacks(l, 0, m, None)
        load_input(lx, 0)

    load_input(la, 0)
    run_layers(sp, dict(o=units), la, lx, prologue, turn, lambda l, b: None)



def experts_block(nc, a, out, x2, ident, ident_bf):
    ctx = ExitStack()
    with ctx:
        def sb(name, shape, dt=F32):
            return ctx.enter_context(nc.sbuf_tensor(name, shape, dt))

        def sem(name):
            return ctx.enter_context(nc.semaphore(name))

        slots_x = nc.dram_tensor("slots_x", [TILES * P, D], F32, kind="Internal").ap()
        slots_y = nc.dram_tensor("slots_y", [TILES * P, D], F32, kind="Internal").ap()
        w = sb("expert_w", [P, NE * WE])
        bias_raw = sb("bias_raw", [NE, BE])
        bias_split = sb("bias_split", [NE, PARTS, BE], BF16)
        bias = sb("bias_rows", [PARTS, NE * BE], BF16)
        wg, bg = sb("wg", [P, 2, NE]), sb("bg", [P, NE])
        ones, tri = sb("ones_bf", [P, P], BF16), sb("tri_bf", [P, P], BF16)
        zeros = sb("zeros", [P, D])
        x2T = sb("x2T", [P, 2 * NT, P])
        counting = sb("counting", [P, TILES], I32)
        count_f, count_128 = sb("count_f", [P, TILES]), sb("count_128", [P, NE])
        logits, best, away = sb("logits", [P, NT, NE]), sb("best", [P, NT, NE]), sb("away", [P, NT, NE])
        expd, total = sb("expd", [P, NT, NE]), sb("total", [P, 2, NT])
        gate, best_at, best_f = sb("gate", [P, NT, 2]), sb("best_at", [P, NT, NE], U32), sb("best_f", [P, NT, 2])
        hot, both = sb("hot", [P, NT, 2, NE]), sb("both", [P, NT, NE], BF16)
        many, tiles_of = sb("many", [P, NE, NE]), sb("tiles_of", [P, NE])
        end, first = sb("end", [P, NE]), sb("first", [P, NE])
        place, place_hot = sb("place", [P, NT, NE]), sb("place_hot", [P, NT, 2, NE])
        slot_f, slot = sb("slot_f", [P, NT, 2]), sb("slot", [P, NT, 2], U32)
        past, expert_f, expert = sb("past", [P, TILES, NE]), sb("expert_f", [P, 2, TILES]), sb("expert", [P, TILES], I32)
        ones_ne = sb("ones_ne", [P, NE])
        gathered = w[:, 0:NT * 2 * D].rearrange("p (t c d) -> p t c d", t=NT, c=2)
        y, stats, mv = x2T[:, :, :].rearrange("p (t k) q -> p t (k q)", k=2), sb("stats_c", [P, NT, 6]), sb("mv_c", [P, NT, 2])
        ve, rstd, neg_half = sb("ve_c", [P, NT]), sb("rstd_c", [P, NT]), sb("neg_half_c", [P, NT])
        lane = [NS(xt=sb(f"xt{i}", [P, D]), xT=sb(f"xT_{i}", [P, 2, P]), h=sb(f"h{i}", [P, FH]),
                   hT=[sb(f"h{l}T_{i}", [P, FH // P, P]) for l in (1, 2)], y=sb(f"y_{i}", [P, D]),
                   bt=ctx.enter_context(nc.psum_tensor(f"bt{i}", [P, 512], F32)),
                   bh=ctx.enter_context(nc.psum_tensor(f"bh{i}", [P, 512], F32)),
                   by=ctx.enter_context(nc.psum_tensor(f"by{i}", [P, 512], F32)),
                   pe=sem(f"lane{i}_pe"), dve=sem(f"lane{i}_dve"), act=sem(f"lane{i}_act"),
                   x_in=sem(f"lane{i}_x_in"), y_out=sem(f"lane{i}_y_out")) for i in range(2)]
        route = ctx.enter_context(nc.psum_tensor("route", [P, 512], F32))
        x_banks = [lane[0].bt, lane[0].bh, lane[1].bt, lane[1].bh]
        small, weights, made, zeroed = sem("small_in"), [sem(f"w{e}_in") for e in range(NE)], sem("made_c"), sem("zeroed")
        bias_done, bias_in, pe_r, chain = sem("bias_done"), sem("bias_in"), sem("pe_route"), sem("chain_c")
        exp_done, routed, scattered, got = sem("exp_done"), sem("routed"), sem("scattered"), sem("gathered_in")
        var_ready, rstd_ready, final, stored = sem("var_c"), sem("rstd_c_ready"), sem("final"), sem("stored")
        hot_ready, away_ready = sem("hot_ready"), sem("away_ready")
        MADE = 6
        block = ctx.enter_context(nc.Block())

        @block.sync
        def _(sp):
            for dst, src in ((wg[:, :, :], a["wg"].rearrange("(k p) e -> p k e", p=P)), (bg[:, :], a["bg"].partition_broadcast(P)),
                             (bias_raw[:, :], a["bias"])):
                sp.dma_start(dst, src).then_inc(small, 16)
            sp.wait_ge(made, MADE)
            sp.dma_start(slots_x.rearrange("(s p) d -> p s d", p=P),
                         zeros[:, :].unsqueeze(1).to_broadcast([P, TILES, D])).then_inc(zeroed, 16)
            for e in range(NE):
                at = 0
                for name, k, n in (("W1", D // P, FH), ("W2", FH // P, FH), ("W3", FH // P, D)):
                    sp.dma_start(w[:, e * WE + at:e * WE + at + k * n].rearrange("p (k n) -> p k n", k=k),
                                 a[name][e, :, :].rearrange("(k p) n -> p k n", p=P)).then_inc(weights[e], 16)
                    at += k * n
                if e == 0:
                    sp.wait_ge(bias_done, 4)
                    for i in range(PARTS):
                        sp.dma_start(bias[i:i + 1, :], bias_split[:, i, :]).then_inc(bias_in, 16)
            sp.wait_ge(scattered, 16 * 2 * NT)

            def load(l, s):
                sp.dma_start(l.xt[:, :], slots_x[bass.ds(s * P, P), :]).then_inc(l.x_in, 16)

            def store(l, s, i):
                sp.wait_ge(l.dve, 4 * i + (4 + 4))
                sp.sem_inc(stored, 1)
                sp.dma_start(slots_y[bass.ds(s * P, P), :], l.y[:, :]).then_inc(l.y_out, 16)

            for n, l in enumerate(lane):
                load(l, n)
            with sp.Fori(0, TILES // 2 - 1) as i:
                for n, l in enumerate(lane):
                    sp.wait_ge(l.pe, 6 * i + 1)
                    sp.sem_inc(stored, 1)
                    load(l, 2 * i + (2 + n))
                for n, l in enumerate(lane):
                    store(l, 2 * i + n, i)
            last = TILES // 2 - 1
            for n, l in enumerate(lane):
                store(l, 2 * last + n, last)
            sp.wait_ge(final, 1)
            sp.dma_start(out.rearrange("b (q p) d -> p (b q) d", p=P), gathered[:, :, 0, :]).then_inc(zeroed, 16)
            sp.wait_ge(zeroed, 32)

        @block.gpsimd
        def _(pool):
            G = nc.gpsimd
            count = Tally(made)

            def did(ins):
                ins.then_inc(made, 1)
                count.n += 1
                pool.wait_ge(made, count.value())

            did(G.memset(zeros[:, :], 0.0))
            did(G.memset(ones[:, :], 1.0))
            did(G.affine_select(out=tri[:, :], in_=ones[:, :], compare_op=ALU.is_gt, fill=0.0, base=0,
                                pattern=[[1, P]], channel_multiplier=-1))
            did(G.iota(counting[:, :], pattern=[[1, TILES]], base=0, channel_multiplier=0))
            did(G.memset(neg_half[:, :], -0.5))
            did(G.memset(ones_ne[:, :], 1.0))
            pool.wait_ge(small, 48)
            for n, ins in enumerate((lambda: G.tensor_copy(bias_split[:, 0, :], bias_raw[:, :]),
                                     lambda: G.tensor_tensor(bias_raw[:, :], bias_raw[:, :], bias_split[:, 0, :], ALU.subtract),
                                     lambda: G.tensor_copy(bias_split[:, 1, :], bias_raw[:, :]),
                                     lambda: G.tensor_tensor(bias_split[:, 2, :], bias_raw[:, :], bias_split[:, 1, :], ALU.subtract))):
                ins().then_inc(bias_done, 1)
                pool.wait_ge(bias_done, n + 1)
            pool.wait_ge(zeroed, 16)
            pool.wait_ge(routed, 1)
            for t in range(NT):
                for c in range(2):
                    G.indirect_dma_start(out=slots_x[:, :], out_offset=bass.IndirectOffsetOnAxis(ap=slot[:, t, c:c + 1], axis=0),
                                         in_=x2[:, t, :], in_offset=None).then_inc(scattered, 16)
            for l in lane:
                pool.wait_ge(l.y_out, 16 * (TILES // 2 + 1))
            for t in range(NT):
                for c in range(2):
                    G.indirect_dma_start(out=gathered[:, t, c, :], out_offset=None, in_=slots_y[:, :],
                                         in_offset=bass.IndirectOffsetOnAxis(ap=slot[:, t, c:c + 1], axis=0)).then_inc(got, 16)
            pool.wait_ge(var_ready, 1)
            G.tensor_tensor(rstd[:, :], ve[:, :], neg_half[:, :], ALU.pow).then_inc(rstd_ready, 1)

        @block.tensor
        def _(pe):
            pe.wait_ge(made, MADE)
            for t in range(NT):
                for k in range(2):
                    last = nc.tensor.transpose(x_banks[t // 2][:, (2 * (t % 2) + k) * P:(2 * (t % 2) + k + 1) * P],
                                               x2[:, t, k * P:(k + 1) * P], ident[:, :])
                if t % 2:
                    last.then_inc(pe_r, 1)
            pe.wait_ge(chain, 4)
            pe.wait_ge(small, 48)
            for t in range(NT):
                for k in range(2):
                    last = nc.tensor.matmul(route[:, t * NE:(t + 1) * NE], x2T[:, 2 * t + k, :], wg[:, k, :],
                                            start=(k == 0), stop=(k == 1))
            last.then_inc(pe_r, 1)
            pe.wait_ge(hot_ready, 1)
            for t in range(NT):
                for before in range(t + 1):
                    nc.tensor.matmul(route[:, 128 + t * NE:128 + (t + 1) * NE], tri[:, :] if before == t else ones[:, :],
                                     both[:, before, :], start=(before == 0), stop=(before == t))
            for t in range(NT):
                last = nc.tensor.matmul(route[:, 256:256 + NE], ones[:, :], both[:, t, :], start=(t == 0), stop=(t == NT - 1))
            last.then_inc(pe_r, 1)
            pe.wait_ge(routed, 1)
            pe.wait_ge(bias_in, 48)
            for e in range(NE):
                pe.wait_ge(weights[e], 48)

            def transposes(l, src, n):
                for k in range(n):
                    last = nc.tensor.transpose(l.bt[:, k * P:(k + 1) * P], src[:, k * P:(k + 1) * P], ident[:, :])
                last.then_inc(l.pe, 1)

            def layer(l, bank, xT, k_tiles, n, e, at, bias_at):
                nc.tensor.matmul(bank[:, 0:n], ones[0:PARTS, :], bias[0:PARTS, bass.ds(e * BE + bias_at, n)], start=True, stop=False)
                for k in range(k_tiles):
                    last = nc.tensor.matmul(bank[:, 0:n], xT[:, k, :], w[:, bass.ds(e * WE + (at + k * n), n)],
                                            start=False, stop=(k == k_tiles - 1))
                last.then_inc(l.pe, 1)

            with pe.Fori(0, TILES // 2) as i:
                es = []
                for n, l in enumerate(lane):
                    es.append(pe.value_load(expert[0:1, bass.ds(2 * i + n, 1)], min_val=0, max_val=NE - 1))
                for l in lane:
                    pe.wait_ge(l.x_in, 16 * i + 16)
                    pe.wait_ge(l.dve, 4 * i + 3)
                    transposes(l, l.xt, 2)
                for l, e in zip(lane, es):
                    pe.wait_ge(l.dve, 4 * i + (4 + 1))
                    pe.wait_ge(l.act, 2 * i + 1)
                    layer(l, l.bh, l.xT, D // P, FH, e, 0, 0)
                for l in lane:
                    pe.wait_ge(l.act, 2 * i + 2)
                    transposes(l, l.h, 4)
                for l, e in zip(lane, es):
                    pe.wait_ge(l.dve, 4 * i + (4 + 2))
                    layer(l, l.bh, l.hT[0], FH // P, FH, e, 2 * FH, FH)
                for l in lane:
                    pe.wait_ge(l.act, 2 * i + 3)
                    transposes(l, l.h, 4)
                for l, e in zip(lane, es):
                    pe.wait_ge(l.dve, 4 * i + (4 + 3))
                    layer(l, l.by, l.hT[1], FH // P, D, e, 6 * FH, 2 * FH)

        @block.scalar
        def _(act):
            for l in lane:
                act.sem_inc(l.act, 1)
            act.wait_ge(away_ready, 1)
            nc.scalar.activation(expd[:, :, :], away[:, :, :], ACT.Exp).then_inc(exp_done, 1)
            with act.Fori(0, TILES // 2) as i:
                for layer in range(2):
                    for l in lane:
                        act.wait_ge(l.pe, 6 * i + (2 + 2 * layer))
                        nc.scalar.activation(l.h[:, :], l.bh[:, :], ACT.Gelu).then_inc(l.act, 1)

        @block.vector
        def _(dve):
            V = nc.vector
            ch = Tally(chain)

            def link(ins):
                ins.then_inc(chain, 1)
                ch.n += 1
                dve.wait_ge(chain, ch.value())

            for l in lane:
                dve.sem_inc(l.dve, 4)
                dve.sem_inc(l.y_out, 16)
            dve.wait_ge(made, MADE)
            for j in range(4):
                dve.wait_ge(pe_r, j + 1)
                V.tensor_copy(x2T[:, 4 * j:4 * j + 4, :].rearrange("p k q -> p (k q)"), x_banks[j][:, :]).then_inc(chain, 1)
                ch.n += 1
            link(V.tensor_copy(count_f[:, :], counting[:, :]))
            link(V.tensor_scalar(count_128[:, :], count_f[:, 0:NE], float(P), None, ALU.mult))
            dve.wait_ge(small, 48)
            dve.wait_ge(pe_r, 5)
            link(V.tensor_tensor(logits[:, :, :], route[:, 0:NT * NE].rearrange("p (t e) -> p t e", t=NT),
                                 bg[:, :].unsqueeze(1).to_broadcast([P, NT, NE]), ALU.add))
            for t in range(NT):
                ins = V.max(best[:, t, :], logits[:, t, :])
            link(ins)
            for t in range(NT):
                ins = V.max_index(best_at[:, t, :], best[:, t, :], logits[:, t, :])
            link(ins)
            V.tensor_tensor(away[:, :, :], best[:, :, :], best[:, :, 0:1].to_broadcast([P, NT, NE]), ALU.subtract).then_inc(away_ready, 1)
            link(V.tensor_copy(best_f[:, :, :], best_at[:, :, 0:2]))
            link(V.tensor_tensor(hot[:, :, :, :], count_f[:, 0:NE].unsqueeze(1).unsqueeze(1).to_broadcast([P, NT, 2, NE]),
                                 best_f[:, :, :].unsqueeze(3).to_broadcast([P, NT, 2, NE]), ALU.is_equal))
            V.tensor_tensor(both[:, :, :], hot[:, :, 0, :], hot[:, :, 1, :], ALU.add).then_inc(hot_ready, 1)
            dve.wait_ge(exp_done, 1)
            link(V.tensor_reduce(total[:, 0, :], expd[:, :, :], X, ALU.add))
            link(V.reciprocal(total[:, 1, :], total[:, 0, :]))
            link(V.tensor_tensor(gate[:, :, :], expd[:, :, 0:2], total[:, 1, :].unsqueeze(2).to_broadcast([P, NT, 2]), ALU.mult))
            dve.wait_ge(pe_r, 6)
            link(V.tensor_tensor(many[:, :, :], route[:, 256:256 + NE].unsqueeze(2).to_broadcast([P, NE, NE]),
                                 count_128[:, :].unsqueeze(1).to_broadcast([P, NE, NE]), ALU.is_gt))
            link(V.tensor_reduce(tiles_of[:, :], many[:, :, :], X, ALU.add))
            link(V.tensor_tensor_scan(end[:, :], ones_ne[:, :], tiles_of[:, :], 0.0, ALU.mult, ALU.add))
            link(V.tensor_tensor(first[:, :], end[:, :], tiles_of[:, :], ALU.subtract))
            link(V.tensor_scalar(tiles_of[:, :], first[:, :], float(P), None, ALU.mult))
            link(V.tensor_tensor(place[:, :, :], route[:, 128:128 + NT * NE].rearrange("p (t e) -> p t e", t=NT),
                                 tiles_of[:, :].unsqueeze(1).to_broadcast([P, NT, NE]), ALU.add))
            link(V.tensor_tensor(place_hot[:, :, :, :], hot[:, :, :, :],
                                 place[:, :, :].unsqueeze(2).to_broadcast([P, NT, 2, NE]), ALU.mult))
            link(V.tensor_reduce(slot_f[:, :, :], place_hot[:, :, :, :], X, ALU.add))
            link(V.tensor_copy(slot[:, :, :], slot_f[:, :, :]))
            link(V.tensor_tensor(past[:, :, :], count_f[:, :].unsqueeze(2).to_broadcast([P, TILES, NE]),
                                 end[:, :].unsqueeze(1).to_broadcast([P, TILES, NE]), ALU.is_ge))
            link(V.tensor_reduce(expert_f[:, 0, :], past[:, :, :], X, ALU.add))
            link(V.tensor_scalar(expert_f[:, 1, :], expert_f[:, 0, :], float(NE - 1), None, ALU.min))
            V.tensor_copy(expert[:, :], expert_f[:, 1, :]).then_inc(routed, 1)
            with dve.Fori(0, TILES // 2) as i:
                for step in range(3):
                    for l in lane:
                        dve.wait_ge(l.pe, 6 * i + (1 + 2 * step))
                        if step == 0:
                            ins = V.tensor_copy(l.xT[:, :, :].rearrange("p k q -> p (k q)"), l.bt[:, 0:D])
                        else:
                            ins = V.tensor_copy(l.hT[step - 1][:, :, :].rearrange("p k q -> p (k q)"), l.bt[:, :])
                        ins.then_inc(l.dve, 1)
                for l in lane:
                    dve.wait_ge(l.pe, 6 * i + 6)
                    dve.wait_ge(l.y_out, 16 * i + 16)
                    V.tensor_copy(l.y[:, :], l.by[:, 0:D]).then_inc(l.dve, 1)
            dve.wait_ge(got, 16 * 2 * NT)
            for c in range(2):
                for t in range(NT):
                    base = x2[:, t, :] if c == 0 else y[:, t, :]
                    ins = V.scalar_tensor_tensor(out=y[:, t, :], in0=gathered[:, t, c, :], scalar=gate[:, t, c:c + 1],
                                                 in1=base, op0=ALU.mult, op1=ALU.add)
                link(ins)
            for t in range(NT):
                ins = V.bn_stats(stats[:, t, :], y[:, t, :])
            link(ins)
            for t in range(NT):
                ins = V.bn_aggr(mv[:, t, :], stats[:, t, :])
            link(ins)
            V.tensor_scalar(ve[:, :], mv[:, :, 1], EPS, None, ALU.add).then_inc(var_ready, 1)
            dve.wait_ge(rstd_ready, 1)
            for t in range(NT):
                ins = V.tensor_scalar(gathered[:, t, 0, :], y[:, t, :], mv[:, t, 0:1], rstd[:, t:t + 1], ALU.subtract, ALU.mult)
            ins.then_inc(final, 1)



def program(nc, a, out):
    ca, cx = finish_shape(self_attention_shape()), finish_shape(cross_attention_shape())
    scratch = {c.name: nc.dram_tensor(f"parts_{c.name}", [2, PARTS, P, S + c.T], BF16, kind="Internal").ap()
               for c in (ca, cx)}
    outer = ExitStack()
    with outer:
        x2, ident, ident_bf = (outer.enter_context(nc.sbuf_tensor(n, sh, dt)) for n, sh, dt in (
            ("x_in_out", [P, NT, D], F32), ("ident", [P, P], F32), ("ident_bf", [P, P], BF16)))
        attention_block(nc, a, ca, cx, scratch, x2, ident, ident_bf)
        experts_block(nc, a, out, x2, ident, ident_bf)


def attention_block(nc, a, ca, cx, scratch, x2, ident, ident_bf):
    ctx = ExitStack()
    with ctx:
        def sb(name, shape, dt=F32):
            return ctx.enter_context(nc.sbuf_tensor(name, shape, dt))

        def ps(name, w):
            return ctx.enter_context(nc.psum_tensor(name, [P, w], F32))

        mbank = [ps(f"m_bank{i}", 512) for i in range(M_RING)]
        stbank = [ps(f"st_bank{i}", 1024) for i in range(ST_RING)]
        obank = ps("o_bank", 512)

        loaded = ctx.enter_context(nc.semaphore("loaded"))
        made = ctx.enter_context(nc.semaphore("made"))
        loaded_cross, made_cross = (ctx.enter_context(nc.semaphore(n)) for n in ("loaded_cross", "made_cross"))
        sa, sx, ring = attention_sems(ctx, nc, ca), attention_sems(ctx, nc, cx), ring_sems(ctx, nc)

        x0 = x2
        x1 = sb("x1", [P, NT, D])
        common = dict(mbank=mbank, stbank=stbank, obank=obank, loaded=loaded, loaded_cross=loaded_cross, made=made, made_cross=made_cross, ident=ident, ident_bf=ident_bf)
        common.update(
            probs=[sb(f"probs{i}", [P, 1024]) for i in range(PROB_RING)],
            mparts=sb("max_parts", [P, 2 * UH, PARTS], BF16), nm=sb("neg_max", [P, 2, 2 * UH]),
            oT_unit=sb("oT_unit", [P, S]), rden=sb("rden", [P, 2, UH]), o_tm=sb("o_tokens", [P, 2, D]),
            oT=sb("oT", [P, 2, S]), y=sb("y", [P, 2, D]), y2=sb("y_biased", [P, 2, D]), stats=sb("stats", [P, 2, 6]),
            mv=sb("mean_var", [P, 2, 2]), ve=sb("var_eps", [P, 2]), rstd=sb("rstd", [P, 2]),
            neg_half=sb("neg_half", [P, 2]), qs=sb("quant_scale", [P, 3, 2]),
            qa=sb("quant_a", [P, 2, D]), qb=sb("quant_b", [P, 2, D]),
            cmask=sb("causal_mask", [P, 2, S]), junk=sb("masked_scores", [P, 2 * UH, S]),
            qst=[sb(f"q_stack{m}", [P, HH, S], BF16) for m in range(2)],
            )
        kst = [sb(f"k_stack{m}", [P, HH, SK], BF16) for m in range(2)]
        vaug = [sb(f"v_ones{m}", [P, len(cx.tiles), HH, VW]) for m in range(2)]
        f = sb("qk_rows", [P, S + SK])
        parts = sb("qk_parts", [P, PARTS, S + SK], BF16)
        parts_sa = sb("qk_parts_self", [P, PARTS, 2 * S], BF16)
        xT = sb("ctxT", [P, 2, SK])
        xTs = sb("xT", [P, 2, S])
        wts = {n: sb(n, [P, 2, D]) for n in ("w_q", "w_k", "w_v", "w_o", "xw_q", "xw_p", "xw_qq", "xw_pq",
                                             "xw_k", "xw_v")}
        bq, bk = sb("bq", [P, 2]), sb("bk", [P, 2])
        bv, bp = sb("bv", [P, D]), sb("bp", [P, D])

        ta = NS(**{**common, "mx": sb("row_max_self", [P, 2 * UH, 1]), "kst": kst, "vaug": vaug, "f": sb("qk_rest", [P, 2 * S]),
                   "parts": parts_sa, "xT": xTs, "wq": wts["w_q"], "wk": wts["w_k"],
                   "wv": wts["w_v"], "wo": wts["w_o"], "x_in": x0, "x_out": x1})
        tx = NS(**{**common, "mx": sb("row_max", [P, 2 * UH, cx.NC]), "kst": kst, "vaug": vaug, "f": f,
                   "parts": parts, "xT": xT, "wq": wts["xw_q"], "wk": wts["xw_k"], "wv": wts["xw_v"],
                   "wo": wts["xw_p"], "wq_raw": wts["xw_q"], "wp_raw": wts["xw_p"], "wq_q": wts["xw_qq"],
                   "wp_q": wts["xw_pq"], "xq": sb("x_quant", [P, 2, D]), "oq": sb("o_quant", [P, 2, D]),
                   "xqT": sb("xqT", [P, 2, S]), "bq": bq, "bk": bk, "bv": bv, "bp": bp, "x_in": x1, "x_out": x2})
        rows = lambda w: w.rearrange("(k p) n -> p k n", p=P)
        loads = [(wts["w_q"], rows(a["w_q"])),
                 (wts["w_k"], rows(a["w_k"])), (wts["w_v"], rows(a["w_v"])), (wts["w_o"], rows(a["w_o"])),
                 (x0, a["x"].rearrange("b (q p) d -> p (b q) d", p=P)),
                 (wts["xw_q"], rows(a["xw_q"])), (wts["xw_p"], rows(a["xw_p"])),
                 (wts["xw_k"], rows(a["xw_kvT"][:, 0:D])), (wts["xw_v"], rows(a["xw_kvT"][:, D:2 * D])),
                 (bq, a["bq"]), (bk, a["bkv"][:, 0:2]), (bv, a["bv"].partition_broadcast(P)), (bp, a["bp"].partition_broadcast(P))]
        SELF_LOADS = 3
        ta.made_all = MADE = 11
        ta.cross_loads = tx.cross_loads = 16 * (len(loads) - SELF_LOADS)
        la = NS(c=ca, s=sa, t=ta, x_dram=a["xT"], scratch=scratch["sa"])
        lx = NS(c=cx, s=sx, t=tx, x_dram=a["ctxT"], scratch=scratch["xa"])
        MADE_FIRST = 7
        block = ctx.enter_context(nc.Block())

        @block.scalar
        def _(act):
            for n, (dst, src) in enumerate(loads):
                act.dma_start(dst[:, :, :] if len(dst.shape) == 3 else dst[:, :], src)\
                    .then_inc(loaded if n < SELF_LOADS else loaded_cross, 16)
            act_attention(nc, act, ring, la, lx)

        @block.gpsimd
        def _(pool):
            G = nc.gpsimd
            count, count_cross = Tally(made), Tally(made_cross)

            def did(ins, count=count):
                ins.then_inc(count.sem, 1)
                count.n += 1
                pool.wait_ge(count.sem, count.value())

            did(G.memset(ident[:, :], 0.0))
            did(G.memset(ident_bf[:, :], 0.0))
            did(G.memset(common["cmask"][:, :, :], 0.0))
            did(G.memset(common["neg_half"][:, :], -0.5))
            for w in (ident, ident_bf):
                did(G.affine_select(out=w[:, :], in_=w[:, :], compare_op=ALU.not_equal, fill=1.0, base=0,
                                pattern=[[-1, P]], channel_multiplier=1))
            did(G.affine_select(out=common["cmask"][:, :, :], in_=common["cmask"][:, :, :], compare_op=ALU.is_ge, fill=MASK,
                            base=0, pattern=[[P, 2], [-1, S]], channel_multiplier=1))
            assert count.n == MADE_FIRST
            for m in range(2):
                did(G.memset(kst[m][MROW:STACK, :, 0:S], 1.0))
                did(G.memset(vaug[m][:, :, :, DH:VW], 1.0))
            assert count.n == MADE
            for m in range(2):
                did(G.memset(kst[m][MROW:STACK, :, S:], 1.0), count_cross)
            pool_attention(nc, pool, ring, la, lx)

        @block.vector
        def _(dve):
            dve.wait_ge(made, MADE_FIRST)
            dve.wait_ge(loaded, 16 * SELF_LOADS)
            dve_attention(nc, dve, ring, la, lx)

        @block.tensor
        def _(pe):
            pe.wait_ge(made, MADE_FIRST)
            pe.wait_ge(loaded, 16 * SELF_LOADS)
            nc.tensor.matmul(obank[:, 0:S], ident[:, :], common["cmask"][:, 0, :], start=True, stop=True)
            pe_attention(nc, pe, ring, la, lx)

        @block.sync
        def _(sp):
            sp_attention(nc, sp, ring, la, lx)


def kernel(**inputs):
    import numpy as np
    import concourse.bacc as bacc
    from concourse import mybir as mb
    from concourse.bass_utils import run_bass_kernel_spmd

    g = {k: np.asarray(v) for k, v in inputs.items()}
    arrays = {
        "x": g["x"], "xT": g["x"].transpose(0, 2, 1), "ctxT": g["ctx_2048"].transpose(0, 2, 1),
        "w_q": g["L0_attn_q_wei"], "w_k": g["L0_attn_k_wei"], "w_v": g["L0_attn_v_wei"], "w_o": g["L0_attn_out_wei"],
        "xw_q": g["L0_xattn_wq"], "xw_p": g["L0_xattn_wp"], "xw_kvT": g["L0_xattn_wkv"].T,
        "bq": g["L0_xattn_bq"].reshape(2, 128).T, "bkv": g["L0_xattn_bkv"].reshape(4, 128).T,
        "W1": g["L0_ffn_W1"], "W2": g["L0_ffn_W2"], "W3": g["L0_ffn_W3"], "wg": g["L0_ffn_Wg"], "bg": g["L0_ffn_bg"],
        "bias": np.concatenate([g["L0_ffn_b1"], g["L0_ffn_b2"], g["L0_ffn_b3"]], axis=1),
        "bv": g["L0_xattn_bkv"][256:], "bp": g["L0_xattn_bp"],
    }
    arrays = {k: np.ascontiguousarray(v) for k, v in arrays.items()}
    nc = bacc.Bacc("TRN2", target_bir_lowering=False, num_devices=1)
    aps = {k: nc.dram_tensor("in_" + k, v.shape, mb.dt.from_np(v.dtype), kind="ExternalInput").ap() for k, v in arrays.items()}
    out = nc.dram_tensor("out_0", (4, 256, 256), mb.dt.float32, kind="ExternalOutput").ap()
    program(nc, aps, out)
    r = run_bass_kernel_spmd(nc, [{"in_" + k: v for k, v in arrays.items()}], core_ids=[0])
    return r.results[0]["out_0"]
```

```python
import concourse.bass as bass
from concourse import mybir
from contextlib import ExitStack

F32 = mybir.dt.float32
BF16 = mybir.dt.bfloat16
I32 = mybir.dt.int32
U32 = mybir.dt.uint32
ALU = mybir.AluOpType
ACT = mybir.ActivationFunctionType
X = mybir.AxisListType.X

B, S, D, H, DH = 4, 256, 256, 16, 16
SK = 1601
P = 128
NT = B * S // P
HH = H // 2
UH = 4
PARTS = 3
Q_PARTS = (0, 1, 2, 0, 1, 0)
K_PARTS = (0, 0, 0, 1, 1, 2)
NPROD = len(Q_PARTS)
MROW = NPROD * DH
STACK = MROW + PARTS
VW = DH + 1
NE, FH = 8, 512
WE = (D * FH + FH * FH + FH * D) // P
BE = FH + FH + D
TILES = 2 * B * S // P + NE
MASK = -66504.0
EPS = 1e-5
ROUND = 12582912.0
M_RING, ST_RING, PROB_RING = 3, 2, 4
PV_LAG = 2


def NS(**named):
    return type("Named", (), named)


class Tally:

    def __init__(self, sem, credit=0):
        self.sem, self.credit, self.n = sem, credit, 0
        self.turn = self.per_turn = 0
        self.marks = {}

    def enter(self, turn, per_turn):
        self.turn, self.per_turn, self.start = turn, per_turn, self.n

    def leave(self, turns):
        assert self.n == self.start + self.per_turn, (self.sem, self.n - self.start, self.per_turn)
        more = (turns - 1) * self.per_turn
        self.n += more
        self.marks = {k: v + more for k, v in self.marks.items()}
        self.turn = 0

    def value(self, more=0):
        return self.turn * self.per_turn + (self.n + more)

    def done(self, more=0):
        return self.turn * self.per_turn + (self.n + more + self.credit)

    def mark(self, what):
        self.marks[what] = self.n

    def marked(self, what):
        return self.turn * self.per_turn + (self.marks[what] + self.credit)


def self_attention_shape():
    c = NS(name="sa", cross=False, T=S, tiles=[P] * (S // P), chunks=[(0, S)])
    c.groups = [[0, 1]]
    return c


def cross_attention_shape():
    c = NS(name="xa", cross=True, T=SK, tiles=[P] * (SK // P) + [SK % P])
    c.chunks = [(i * 400 + min(i, 1), 401 if i == 0 else 400) for i in range(4)]
    assert c.chunks[-1][0] + c.chunks[-1][1] == SK
    c.groups = [list(range(i, min(i + 4, len(c.tiles)))) for i in range(0, len(c.tiles), 4)]
    return c


def finish_shape(c):
    c.NC = len(c.chunks)
    c.max_jobs = 2 * UH * c.NC
    c.vjobs = -(-len(c.tiles) // 4)
    c.kjobs = 2 if c.cross else 0
    c.st_unit = UH * len(c.groups)
    jobs = (2 + c.cross) + 2 * c.vjobs + 4 * (1 + c.max_jobs) + 2
    c.pad = -jobs % M_RING
    st_turn, pv_turn = 2 * c.kjobs + 4 * (c.st_unit + 1), 4 * c.st_unit
    assert st_turn % ST_RING == 0 and pv_turn % PROB_RING == 0
    c.chain_turn = 4 * 4 + 4 + (6 + 6 + 3 if c.cross else 2 + 2)
    c.turn = dict(m=jobs + c.pad, st=st_turn, o=4, pv=pv_turn, rows=4, chain=c.chain_turn)
    return c


def split_at(c):
    return c.st_unit // 2


def plan(c, after, pending, output):
    ns = c.st_unit
    jobs = [[] for _ in range(ns)]
    if after:
        slots = ns - 1 - ns // 8
        for i in range(after.max_jobs):
            jobs[i * slots // after.max_jobs].append("max")
    if pending:
        jobs[max(1, len(c.groups) - 1)].append("o")
    if output:
        jobs[ns - 3 if ns > 4 else 2].append("output_transposes")
    if after:
        jobs[ns - 1].append("rows")
    if output:
        jobs[ns - 1].append("output_product")
    return jobs


def attention_sems(ctx, nc, c):
    names = ("w_ready xq_ready oq_ready q_taken rest_ready middle_ready parts_ready scratch_written stack0_loaded stack1_loaded "
             "x_loaded x_used var_ready rstd_ready")
    return NS(**{n: ctx.enter_context(nc.semaphore(f"{c.name}_{n}")) for n in names.split()})


def ring_sems(ctx, nc):
    names = "m_full m_free st_full act_done o_free pv_done rows_ready masked normalised dve_chain turnstile"
    return NS(**{n: ctx.enter_context(nc.semaphore(n)) for n in names.split()})


def run_layers(eng, tallies, la, lx, prologue, turn, final):
    prologue(la)
    for l in (la, lx):
        with eng.Fori(0, B - 1) as b:
            for name, x in tallies.items():
                x.enter(b, l.c.turn[name])
            turn(l, b, l, b + 1)
        for x in tallies.values():
            x.leave(B - 1)
        if l is la:
            turn(la, B - 1, lx, 0)
    final(lx, B - 1)



def pe_attention(nc, pe, r, la, lx):
    mt = Tally(r.m_free, M_RING)
    st = Tally(r.act_done, ST_RING)
    ot = Tally(r.o_free, 1)
    pt = Tally(r.pv_done, PROB_RING)
    mp = Tally(r.rows_ready)
    t = la.t
    late = []

    def m_bank():
        pe.wait_ge(mt.sem, mt.value(1))
        return t.mbank[mt.n % M_RING]

    def m_done(last, n=1):
        last.then_inc(r.m_full, n)
        mt.n += n

    def transposes(src, ready=None):
        bank = m_bank()
        if ready is not None:
            pe.wait_ge(*ready)
        for tt in range(2):
            for k in range(2):
                last = nc.tensor.transpose(bank[:, (2 * k + tt) * P:(2 * k + tt + 1) * P],
                                           src[:, tt, k * P:(k + 1) * P], t.ident[:, :])
        m_done(last)

    def project_k(l, b, m):
        c, t = l.c, l.t
        pe.wait_ge(l.s.x_loaded, b * 16 + 16)
        ms = slice(m * P, (m + 1) * P)
        for pair in ((0, 1), (2, 3))[:c.kjobs]:
            pe.wait_ge(st.sem, st.value(1))
            bank = t.stbank[st.n % ST_RING]
            for i, ch in enumerate(pair):
                a, w = c.chunks[ch]
                for k in range(2):
                    last = nc.tensor.matmul(bank[:, i * 512:i * 512 + w], t.wk[:, k, ms], t.xT[:, k, a:a + w],
                                            start=(k == 0), stop=(k == 1))
            last.then_inc(r.st_full, 1)
            st.n += 1

    def x_transposes(l, b):
        transposes(l.t.xq, (l.s.xq_ready, b + 1))
        mt.mark("xqT")

    def project_q(l, m):
        c, t = l.c, l.t
        ms = slice(m * P, (m + 1) * P)
        if c.cross and m == 0:
            pe.wait_ge(mt.sem, mt.marked("xqT"))
        bank = m_bank()
        for k in range(2):
            rhs = t.xqT[:, k, :] if c.cross else t.xT[:, k, :]
            last = nc.tensor.matmul(bank[:, 0:S], t.wq[:, k, ms], rhs, start=(k == 0), stop=(k == 1))
        if not c.cross:
            for k in range(2):
                last = nc.tensor.matmul(bank[:, S:2 * S], t.wk[:, k, ms], t.xT[:, k, :], start=(k == 0), stop=(k == 1))
        m_done(last)

    def project_qk(l, b, m):
        project_k(l, b, m)
        if l.c.cross and m == 0:
            x_transposes(l, b)
        project_q(l, m)

    def project_v(l, b, m):
        c, t = l.c, l.t
        for v in range(c.vjobs):
            bank = m_bank()
            for i, kt in enumerate(range(4 * v, min(4 * v + 4, len(c.tiles)))):
                n = c.tiles[kt]
                for k in range(2):
                    last = nc.tensor.matmul(bank[0:n, i * P:(i + 1) * P], t.xT[:, k, kt * P:kt * P + n],
                                            t.wv[:, k, m * P:(m + 1) * P], start=(k == 0), stop=(k == 1))
            m_done(last)

    def between_steps(project, l, b, m):
        if l.c.cross:
            flush()
        project(l, b, m)
        flush()

    def stack_loaded(l, b, m):
        pe.wait_ge((l.s.stack0_loaded, l.s.stack1_loaded)[m], b * 192 + 192)

    def max_jobs(l, unit):
        m, g = unit
        for j in range(UH):
            h = UH * g + j
            for qt in range(2):
                for a, w in l.c.chunks:
                    bank = m_bank()
                    m_done(nc.tensor.matmul(bank[:, 0:w], t.qst[m][0:MROW, h, qt * P:(qt + 1) * P],
                                            t.kst[m][0:MROW, h, a:a + w], start=True, stop=True))
                    yield

    def rows_of_max():
        pe.wait_ge(mp.sem, mp.value(1))
        mp.n += 1
        pe.wait_ge(st.sem, st.value(1))
        bank = t.stbank[st.n % ST_RING]
        for u in range(2 * UH):
            last = nc.tensor.matmul(bank[MROW:STACK, u * P:(u + 1) * P], t.mparts[:, u, :], t.ident_bf[:, :],
                                    start=True, stop=True)
        last.then_inc(r.st_full, 1)
        st.n += 1
        st.mark("rows")

    def pv(l, unit, j, grp, n_st, first, final):
        m, g = unit
        h = UH * g + j
        if first:
            pe.wait_ge(ot.sem, ot.value(1))
        if l.c.cross:
            pe.wait_ge(r.act_done, st.turn * st.per_turn + (n_st + 1 + ST_RING))
        else:
            pe.wait_ge(r.masked, pt.value(1))
        slot = t.probs[pt.n % PROB_RING]
        tiles = l.c.tiles
        for i, kt in enumerate(grp):
            n = tiles[kt]
            last = nc.tensor.matmul(t.obank[32 * j:32 * j + VW, 0:S], t.vaug[m][0:n, kt, h, :],
                                    slot[0:n, i * S:(i + 1) * S], start=(kt == 0), stop=(kt == len(tiles) - 1))
        last.then_inc(r.pv_done, 1)
        pt.n += 1
        if final:
            ot.n += 1

    def flush():
        while late:
            pv(*late.pop(0))

    def o_transposes():
        bank = m_bank()
        pe.wait_ge(ot.sem, ot.done())
        for qt in range(2):
            last = nc.tensor.transpose(bank[:, qt * P:(qt + 1) * P], t.oT_unit[:, qt * P:(qt + 1) * P], t.ident[:, :])
        m_done(last)

    def output_transposes(l, b):
        if l.c.cross:
            transposes(l.t.oq, (l.s.oq_ready, b + 1))
        else:
            pe.wait_ge(mt.sem, mt.marked("o"))
            transposes(l.t.o_tm)
        mt.mark("oT")

    def output_product(l):
        pe.wait_ge(mt.sem, mt.marked("oT"))
        bank = m_bank()
        for tt in range(2):
            for k in range(2):
                last = nc.tensor.matmul(bank[:, tt * D:(tt + 1) * D], t.oT[:, k, tt * P:(tt + 1) * P], l.t.wo[:, k, :],
                                        start=(k == 0), stop=(k == 1))
        m_done(last, 1 + l.c.pad)

    def step(l, unit, after, pending, output=None):
        c = l.c
        m, g = unit
        more = max_jobs(*after) if after else iter(())
        pe.wait_ge(st.sem, st.marked("rows"))
        i = 0
        jobs = plan(c, after and after[0].c, pending, output)
        for j in range(UH):
            h = UH * g + j
            for gi, grp in enumerate(c.groups):
                pe.wait_ge(st.sem, st.value(1))
                bank = t.stbank[st.n % ST_RING]
                for k, kt in enumerate(grp):
                    n = c.tiles[kt]
                    last = nc.tensor.matmul(bank[0:n, k * S:(k + 1) * S], t.kst[m][0:STACK, h, kt * P:kt * P + n],
                                            t.qst[m][0:STACK, h, :], start=True, stop=True)
                last.then_inc(r.st_full, 1)
                late.append((l, unit, j, grp, st.n, j == 0 and gi == 0, i == c.st_unit - 1))
                st.n += 1
                if i == 0:
                    while len(late) > 1:
                        pv(*late.pop(0))
                for job in jobs[i]:
                    if job == "max":
                        next(more)
                    elif job == "o":
                        o_transposes()
                        mt.mark("o")
                    elif job == "output_transposes":
                        output_transposes(*output)
                    elif job == "rows":
                        rows_of_max()
                    else:
                        output_product(output[0])
                if len(late) > PV_LAG:
                    pv(*late.pop(0))
                i += 1

    def turn(l, b, ln, bn):
        between_steps(project_qk, ln, bn, 0)
        stack_loaded(l, b, 1)
        step(l, (0, 1), (l, (1, 0)), True)
        between_steps(project_v, ln, bn, 0)
        step(l, (1, 0), (l, (1, 1)), True)
        between_steps(project_qk, ln, bn, 1)
        if ln is not l:
            pe.wait_ge(t.made_cross, 1)
            pe.wait_ge(t.made_stack0, 1)
        stack_loaded(ln, bn, 0)
        step(l, (1, 1), (ln, (0, 0)), True)
        between_steps(project_v, ln, bn, 1)
        step(ln, (0, 0), (ln, (0, 1)), True, (l, b))
        flush()

    def prologue(l):
        project_qk(l, 0, 0)
        project_v(l, 0, 0)
        project_qk(l, 0, 1)
        pe.wait_ge(t.loaded_cross, t.cross_loads)
        transposes(lx.t.wq_q, (lx.s.w_ready, 1))
        transposes(lx.t.wp_q, (lx.s.w_ready, 2))
        pe.wait_ge(t.made, t.made_all)
        stack_loaded(l, 0, 0)
        for _ in max_jobs(l, (0, 0)):
            pass
        project_v(l, 0, 1)
        rows_of_max()
        step(l, (0, 0), (l, (0, 1)), False)
        flush()

    def final(l, b):
        stack_loaded(l, b, 1)
        step(l, (0, 1), (l, (1, 0)), True)
        step(l, (1, 0), (l, (1, 1)), True)
        step(l, (1, 1), None, True)
        flush()
        o_transposes()
        output_transposes(l, b)
        output_product(l)

    pe.sem_inc(r.pv_done, PROB_RING)
    run_layers(pe, dict(m=mt, st=st, o=ot, pv=pt, rows=mp), la, lx, prologue, turn, final)



def dve_attention(nc, dve, r, la, lx):
    V = nc.vector
    mt = Tally(r.m_full)
    ot = Tally(r.pv_done, PROB_RING)
    ch = Tally(r.dve_chain)
    t = la.t

    def link(ins, plain=False):
        ins.then_inc(r.dve_chain, 1)
        ch.n += 1
        dve.wait_ge(ch.sem, ch.value())
        if plain:
            dve.sem_inc(r.turnstile, 1)

    def job(plain=False):
        dve.wait_ge(mt.sem, mt.value(1))
        if plain:
            dve.sem_inc(r.turnstile, 1)
        return t.mbank[mt.n % M_RING]

    def free(ins, n=1):
        ins.then_inc(r.m_free, n)
        mt.n += n

    def settled():
        dve.wait_ge(r.m_free, mt.value() + M_RING)

    def quantise(src, dst, ready):
        for _ in quantise_steps(src, dst, ready):
            pass

    def quantise_steps(src, dst, ready):
        t = lx.t
        link(V.tensor_reduce(t.qs[:, 0, :], src, X, ALU.max, apply_absolute_value=True))
        yield
        link(V.tensor_scalar(t.qs[:, 1, :], t.qs[:, 0, :], 1.0 / 127.0, 1e-8, ALU.mult, ALU.max))
        yield
        link(V.reciprocal(t.qs[:, 2, :], t.qs[:, 1, :]))
        yield
        scale, inverse = (t.qs[:, i, :].unsqueeze(2).to_broadcast([P, 2, D]) for i in (1, 2))
        link(V.tensor_tensor(t.qa[:, :, :], src, inverse, ALU.mult))
        yield
        link(V.tensor_scalar(t.qb[:, :, :], t.qa[:, :, :], ROUND, -ROUND, ALU.add, ALU.add))
        yield
        link(V.tensor_scalar(t.qa[:, :, :], t.qb[:, :, :], 127.0, -127.0, ALU.min, ALU.max))
        yield
        V.tensor_tensor(dst, t.qa[:, :, :], scale, ALU.mult).then_inc(ready, 1)

    def take_transposed(dst):
        bank = job()
        free(V.tensor_copy(dst.rearrange("p k t -> p (k t)"), bank[:, 0:2 * D]))

    def quantise_x(l, b):
        s, t = l.s, l.t
        dve.wait_ge(r.normalised, b + 2)
        if not (isinstance(b, int) and b == 0):
            dve.wait_ge(s.xq_ready, b)
        yield from quantise_steps(t.x_in[:, bass.ds(2 * b, 2), :], t.xq[:, :, :], s.xq_ready)

    def take_qk(l, b, m):
        if l.c.cross and m == 0:
            for _ in quantise_x(l, b):
                pass
            take_transposed(l.t.xqT)
        take_q(l, b, m)

    def take_q(l, b, m):
        s, t = l.s, l.t
        again = not (isinstance(b, int) and b == 0 and m == 0)
        if l.c.cross:
            bank = job()
            if again:
                dve.wait_ge(s.scratch_written, 32 * b + 16 * m)
            V.tensor_scalar(t.parts[:, 0, 0:S], bank[:, 0:S], t.bq[:, m:m + 1], None, ALU.add)
            free(V.tensor_scalar(t.f[:, 0:S], bank[:, 0:S], t.bq[:, m:m + 1], None, ALU.add))
            settled()
            dve.sem_inc(s.q_taken, 1)
        else:
            bank = job()
            if again:
                dve.wait_ge(s.scratch_written, 32 * b + 16 * m)
            link(V.tensor_copy(t.parts[:, 0, :], bank[:, :]))
            free(V.tensor_tensor(t.f[:, :], bank[:, :], t.parts[:, 0, :], ALU.subtract))
            settled()
            dve.sem_inc(s.q_taken, 1)

    def take_v(l, b, m):
        c, t = l.c, l.t
        for v in range(c.vjobs):
            tiles = c.tiles[4 * v:4 * v + 4]
            n, k = tiles[0], len(tiles)
            bank = job()
            src = bank[0:n, 0:k * P].rearrange("p (k h d) -> p k h d", k=k, h=HH)
            dst = t.vaug[m][0:n, 4 * v:4 * v + k, :, 0:DH]
            if c.cross:
                for i in range(k):
                    bias = t.bv[0:n, m * P:(m + 1) * P].rearrange("p (h d) -> p h d", h=HH)
                    ins = V.tensor_tensor(dst[:, i], src[:, i], bias, ALU.add)
                free(ins)
            else:
                free(V.tensor_copy(dst, src))
        if m == 1:
            settled()
            dve.sem_inc(l.s.x_used, 1)

    def max_jobs(l, unit):
        t = l.t
        settled()
        for u in range(2 * UH):
            for i, (a, w) in enumerate(l.c.chunks):
                bank = job(plain=not l.c.cross)
                if l.c.cross:
                    free(V.reduce_max(t.mx[:, u, i:i + 1], bank[:, 0:w], X))
                else:
                    free(V.tensor_tensor_reduce(out=t.junk[:, u, :], in0=bank[:, 0:S], in1=t.cmask[:, u % 2, :],
                                                scale=1.0, scalar=-3.0e38, op0=ALU.add, op1=ALU.max,
                                                accum_out=t.mx[:, u, i:i + 1]))
                if u < 2 * UH - 1 or i < l.c.NC - 1:
                    yield
        settled()
        link(V.tensor_reduce(t.nm[:, 0, :], t.mx[:, :, :], X, ALU.max, negate=True))
        link(V.tensor_copy(t.mparts[:, :, 0], t.nm[:, 0, :]))
        link(V.tensor_tensor(t.nm[:, 1, :], t.nm[:, 0, :], t.mparts[:, :, 0], ALU.subtract))
        link(V.tensor_copy(t.mparts[:, :, 1], t.nm[:, 1, :]))
        V.tensor_tensor(t.mparts[:, :, 2], t.nm[:, 1, :], t.mparts[:, :, 1], ALU.subtract).then_inc(r.rows_ready, 1)
        yield

    def copy_o(l):
        ot.n += l.c.st_unit
        dve.wait_ge(ot.sem, ot.done())
        V.tensor_copy(t.oT_unit[:, :], t.obank[:, 0:S]).then_inc(r.o_free, 1)

    def take_o(unit):
        m, g = unit
        bank = job()
        v = bank[:, 0:2 * P].rearrange("p (q j w) -> p q j w", q=2, j=UH)
        settled()
        link(V.reciprocal(t.rden[:, :, :], v[:, :, :, DH]))
        a = (m * HH + g * UH) * DH
        dst = t.o_tm[:, :, a:a + UH * DH].rearrange("p q (j d) -> p q j d", j=UH)
        free(V.tensor_tensor(dst, v[:, :, :, 0:DH], t.rden[:, :, :].unsqueeze(3).to_broadcast([P, 2, UH, DH]), ALU.mult))

    def step(l, unit, after, pending, output=None):
        more = max_jobs(*after) if after else iter(())
        quant = iter(())
        for jobs in plan(l.c, after and after[0].c, pending, output):
            for n, job_name in enumerate(jobs):
                if job_name == "max":
                    next(more)
                    if n % 2:
                        next(quant, None)
                elif job_name == "o":
                    take_o(pending)
                    if output and output[0].c.cross:
                        settled()
                        quant = quantise_steps(t.o_tm[:, :, :], lx.t.oq[:, :, :], lx.s.oq_ready)
                elif job_name == "output_transposes":
                    for _ in quant:
                        pass
                    take_transposed(t.oT)
        copy_o(l)
        if output:
            take_output(*output)

    def take_output(l, b):
        s, t = l.s, l.t
        dve.wait_ge(r.normalised, (B if l.c.cross else 0) + b + 1)
        bank = job()
        out = bank[:, 0:2 * D].rearrange("p (q d) -> p q d", q=2)
        free(V.tensor_tensor(t.y[:, :, :], out, t.x_in[:, bass.ds(2 * b, 2), :], ALU.add), 1 + l.c.pad)
        settled()
        y = t.y
        if l.c.cross:
            link(V.tensor_tensor(t.y2[:, :, :], t.y[:, :, :], t.bp[:, :].unsqueeze(1).to_broadcast([P, 2, D]), ALU.add))
            y = t.y2
        for q in range(2):
            ins = V.bn_stats(t.stats[:, q, :], y[:, q, :])
        link(ins, plain=True)
        for q in range(2):
            ins = V.bn_aggr(t.mv[:, q, :], t.stats[:, q, :])
        link(ins)
        V.tensor_scalar(t.ve[:, 1, :], t.mv[:, :, 0], -1.0, None, ALU.mult)
        V.tensor_scalar(t.ve[:, 0, :], t.mv[:, :, 1], EPS, None, ALU.add).then_inc(s.var_ready, 1)

    def turn(l, b, ln, bn):
        take_qk(ln, bn, 0)
        step(l, (0, 1), (l, (1, 0)), (0, 0))
        take_v(ln, bn, 0)
        step(l, (1, 0), (l, (1, 1)), (0, 1))
        take_qk(ln, bn, 1)
        step(l, (1, 1), (ln, (0, 0)), (1, 0))
        take_v(ln, bn, 1)
        step(ln, (0, 0), (ln, (0, 1)), (1, 1), (l, b))

    def prologue(l):
        take_qk(l, 0, 0)
        take_v(l, 0, 0)
        take_qk(l, 0, 1)
        dve.wait_ge(t.loaded_cross, t.cross_loads)
        quantise(lx.t.wq_raw[:, :, :], lx.t.wq_q[:, :, :], lx.s.w_ready)
        quantise(lx.t.wp_raw[:, :, :], lx.t.wp_q[:, :, :], lx.s.w_ready)
        take_transposed(lx.t.wq)
        take_transposed(lx.t.wo)
        for _ in max_jobs(l, (0, 0)):
            pass
        take_v(l, 0, 1)
        step(l, (0, 0), (l, (0, 1)), None)

    def final(l, b):
        step(l, (0, 1), (l, (1, 0)), (0, 0))
        step(l, (1, 0), (l, (1, 1)), (0, 1))
        step(l, (1, 1), None, (1, 0))
        take_o((1, 1))
        settled()
        quantise(t.o_tm[:, :, :], l.t.oq[:, :, :], l.s.oq_ready)
        take_transposed(t.oT)
        take_output(l, b)

    dve.sem_inc(r.m_free, M_RING)
    dve.sem_inc(r.o_free, 1)
    dve.sem_inc(r.normalised, 1)
    run_layers(dve, dict(m=mt, pv=ot, chain=ch), la, lx, prologue, turn, final)



def act_attention(nc, act, r, la, lx):
    st = Tally(r.st_full)
    pt = Tally(r.pv_done, PROB_RING)

    def take_k(l, b, m):
        c, t = l.c, l.t
        if not c.cross:
            act.wait_ge(l.s.q_taken, 2 * b + (m + 1))
            nc.scalar.activation(t.parts[:, 1, :], t.f[:, :], ACT.Identity).then_inc(l.s.middle_ready, 1)
        for pair in ((0, 1), (2, 3))[:c.kjobs]:
            act.wait_ge(st.sem, st.value(1))
            if not (isinstance(b, int) and b == 0 and m == 0):
                act.wait_ge(l.s.scratch_written, 32 * b + 16 * m)
            bank = t.stbank[st.n % ST_RING]
            for i, chunk in enumerate(pair):
                a, w = c.chunks[chunk]
                for dst in (t.f, t.parts[:, 0, :]):
                    last = nc.scalar.activation(dst[:, S + a:S + a + w], bank[:, i * 512:i * 512 + w], ACT.Identity,
                                                bias=t.bk[:, m:m + 1])
            last.then_inc(r.act_done, 1)
            st.n += 1

    def normalise(l, b):
        t = l.t
        y = t.y2 if l.c.cross else t.y
        act.wait_ge(l.s.rstd_ready, 2 * b + 2)
        for q in range(2):
            ins = nc.scalar.activation(t.x_out[:, 2 * b + q, :], y[:, q, :], ACT.Identity,
                                       scale=t.rstd[:, 0, q:q + 1], bias=t.rstd[:, 1, q:q + 1])
        ins.then_inc(r.normalised, 1)

    def middle_parts(l, b, m):
        if l.c.cross:
            act.wait_ge(l.s.rest_ready, 2 * b + (m + 1))
            nc.scalar.activation(l.t.parts[:, 1, :], l.t.f[:, :], ACT.Identity).then_inc(l.s.middle_ready, 1)

    def rows_of_max(unit):
        m, g = unit
        act.wait_ge(st.sem, st.value(1))
        nc.scalar.activation(la.t.qst[m][MROW:STACK, UH * g:UH * (g + 1), :],
                             la.t.stbank[st.n % ST_RING][MROW:STACK, 0:UH * S].rearrange("p (h q) -> p h q", h=UH),
                             ACT.Identity).then_inc(r.act_done, 1)
        st.n += 1

    def step(l, after, split=None):
        c, t = l.c, l.t
        for i in range(c.st_unit):
            act.wait_ge(st.sem, st.value(1))
            act.wait_ge(pt.sem, pt.value(1))
            grp = c.groups[i % len(c.groups)]
            n, w = c.tiles[grp[0]], len(grp) * S
            nc.scalar.activation(t.probs[pt.n % PROB_RING][0:n, 0:w], t.stbank[st.n % ST_RING][0:n, 0:w],
                                 ACT.Exp, scale=float(DH) ** -0.5).then_inc(r.act_done, 1)
            st.n += 1
            pt.n += 1
            if split and i == split_at(l.c):
                middle_parts(*split)
        if after:
            rows_of_max(after)

    def turn(l, b, ln, bn):
        take_k(ln, bn, 0)
        step(l, (1, 0), (ln, bn, 0))
        step(l, (1, 1))
        take_k(ln, bn, 1)
        step(l, (0, 0), (ln, bn, 1))
        step(ln, (0, 1))
        normalise(l, b)

    def prologue(l):
        take_k(l, 0, 0)
        take_k(l, 0, 1)
        ones = l.t.kst[0][MROW:STACK]
        act.wait_ge(l.t.made, l.t.made_all)
        nc.scalar.activation(ones[:, :, S:], ones[:, 0:1, 0:1].to_broadcast([PARTS, HH, SK - S]), ACT.Identity)\
            .then_inc(l.t.made_stack0, 1)
        rows_of_max((0, 0))
        step(l, (0, 1))
        act.wait_ge(l.t.loaded_cross, l.t.cross_loads)

    def final(l, b):
        for after in ((1, 0), (1, 1), None):
            step(l, after)
        normalise(l, b)

    act.sem_inc(r.act_done, ST_RING)
    run_layers(act, dict(st=st, pv=pt), la, lx, prologue, turn, final)



def pool_attention(nc, pool, r, la, lx, fill_rest):
    G = nc.gpsimd
    st = Tally(r.act_done, ST_RING)
    pt = Tally(None)

    def split(l, b, m):
        s, t = l.s, l.t
        if not l.c.cross:
            third_parts(l, b, m)
            return
        pool.wait_ge(s.q_taken, 2 * b + (m + 1))
        st.n += l.c.kjobs
        pool.wait_ge(st.sem, st.done())
        pool.sem_inc(r.turnstile, 1)
        G.tensor_tensor(t.f[:, :], t.f[:, :], t.parts[:, 0, :], ALU.subtract).then_inc(s.rest_ready, 1)

    def third_parts(l, b, m):
        s, t = l.s, l.t
        pool.wait_ge(s.middle_ready, 2 * b + (m + 1))
        pool.sem_inc(r.turnstile, 1)
        G.tensor_tensor(t.parts[:, 2, :], t.f[:, :], t.parts[:, 1, :], ALU.subtract).then_inc(s.parts_ready, 1)
        pool.wait_ge(s.parts_ready, 2 * b + (m + 1))
        pool.sem_inc(r.turnstile, 1)

    def step(l, split=None):
        t = l.t
        for i in range(l.c.st_unit):
            st.n += 1
            if not l.c.cross:
                pool.wait_ge(st.sem, st.done())
                pool.sem_inc(r.turnstile, 1)
                slot = t.probs[pt.n % PROB_RING][:, 0:2 * S].rearrange("p (k q) -> p k q", k=2)
                G.affine_select(out=slot, in_=slot, compare_op=ALU.is_ge, fill=0.0, base=0,
                                pattern=[[-P, 2], [1, S]], channel_multiplier=-1).then_inc(r.masked, 1)
            pt.n += 1
            if split and split[0].c.cross and i == split_at(l.c):
                third_parts(*split)
        st.n += 1

    def rstd(l, b):
        t = l.t
        pool.wait_ge(l.s.var_ready, b + 1)
        G.tensor_tensor(t.rstd[:, 0, :], t.ve[:, 0, :], t.neg_half[:, :], ALU.pow).then_inc(l.s.rstd_ready, 1)
        pool.wait_ge(l.s.rstd_ready, 2 * b + 1)
        G.tensor_tensor(t.rstd[:, 1, :], t.ve[:, 1, :], t.rstd[:, 0, :], ALU.mult).then_inc(l.s.rstd_ready, 1)

    def prologue(l):
        for m in range(2):
            split(l, 0, m)
        fill_rest()
        st.n += 1
        step(l)

    def turn(l, b, ln, bn):
        split(ln, bn, 0)
        step(l, (ln, bn, 0))
        step(l)
        split(ln, bn, 1)
        step(l, (ln, bn, 1))
        step(ln)
        rstd(l, b)

    def final(l, b):
        for _ in range(3):
            step(l)
        rstd(l, b)

    run_layers(pool, dict(st=st, pv=pt), la, lx, prologue, turn, final)



def sp_attention(nc, sp, r, la, lx, fill_for_experts):
    units = Tally(r.o_free, 1)

    def load_input(l, b):
        sp.dma_start(l.t.xT[:, :, :], l.x_dram[b, :, :].rearrange("(k p) t -> p k t", p=P)).then_inc(l.s.x_loaded, 16)

    def stacks(l, b, m, units_done):
        c, s, t, scratch = l.c, l.s, l.t, l.scratch
        sp.wait_ge(s.parts_ready, 2 * b + (m + 1))
        sp.sem_inc(r.turnstile, 1)
        sems = (s.stack0_loaded, s.stack1_loaded)
        if not (isinstance(b, int) and b == 0):
            sp.wait_ge(sems[m], 192 * b)
        sp.dma_start(scratch[m, :, :, :].rearrange("s f t -> f s t"), t.parts[:, :, :]).then_inc(s.scratch_written, 16)
        sp.wait_ge(s.scratch_written, 32 * b + (16 * m + 16))
        sp.sem_inc(r.turnstile, 1)
        if units_done is not None:
            sp.wait_ge(r.o_free, units_done)
        for i in range(NPROD):
            rows = slice(i * DH, (i + 1) * DH)
            sp.dma_start(t.kst[m][rows, :, 0:c.T], scratch[m, K_PARTS[i], :, S:].rearrange("(j d) t -> d j t", d=DH))\
                .then_inc(sems[m], 16)
            sp.dma_start(t.qst[m][rows, :, :], scratch[m, Q_PARTS[i], :, 0:S].rearrange("(j d) t -> d j t", d=DH))\
                .then_inc(sems[m], 16)

    def turn(l, b, ln, bn):
        if ln is l:
            sp.wait_ge(l.s.x_used, b + 1)
            sp.sem_inc(r.turnstile, 1)
            load_input(ln, bn)
        stacks(ln, bn, 0, units.done(2))
        stacks(ln, bn, 1, units.done(4))
        units.n += 4
        if ln is not l:
            fill_for_experts()

    def prologue(l):
        for m in range(2):
            stacks(l, 0, m, None)

    load_input(la, 0)
    run_layers(sp, dict(o=units), la, lx, prologue, turn, lambda l, b: None)



def experts_block(nc, a, out, x2, ident, slots_x, bias_parts):
    ctx = ExitStack()
    with ctx:
        def sb(name, shape, dt=F32):
            return ctx.enter_context(nc.sbuf_tensor(name, shape, dt))

        def sem(name):
            return ctx.enter_context(nc.semaphore(name))

        slots_y = nc.dram_tensor("slots_y", [TILES * P, D], F32, kind="Internal").ap()
        w = sb("expert_w", [P, NE * WE])
        bias = sb("bias_rows", [PARTS, NE * BE], BF16)
        wg, bg = sb("wg", [P, 2, NE]), sb("bg", [P, NE])
        ones, tri = sb("ones_bf", [P, P], BF16), sb("tri_bf", [P, P], BF16)
        x2T = sb("x2T", [P, 2 * NT, P])
        counting = sb("counting", [P, TILES], I32)
        count_f, count_128 = sb("count_f", [P, TILES]), sb("count_128", [P, NE])
        logits, best, away = sb("logits", [P, NT, NE]), sb("best", [P, NT, NE]), sb("away", [P, NT, NE])
        expd, total = sb("expd", [P, NT, NE]), sb("total", [P, 2, NT])
        gate, best_at, best_f = sb("gate", [P, NT, 2]), sb("best_at", [P, NT, NE], U32), sb("best_f", [P, NT, 2])
        hot, both = sb("hot", [P, NT, 2, NE]), sb("both", [P, NT, NE], BF16)
        many, tiles_of = sb("many", [P, NE, NE]), sb("tiles_of", [P, NE])
        end, first = sb("end", [P, NE]), sb("first", [P, NE])
        place, place_hot = sb("place", [P, NT, NE]), sb("place_hot", [P, NT, 2, NE])
        slot_f, slot = sb("slot_f", [P, NT, 2]), sb("slot", [P, NT, 2], U32)
        past, expert_f, expert = sb("past", [P, TILES, NE]), sb("expert_f", [P, 2, TILES]), sb("expert", [P, TILES], I32)
        ones_ne = sb("ones_ne", [P, NE])
        gathered = w[:, 0:NT * 2 * D].rearrange("p (t c d) -> p t c d", t=NT, c=2)
        y, stats, mv = x2T[:, :, :].rearrange("p (t k) q -> p t (k q)", k=2), sb("stats_c", [P, NT, 6]), sb("mv_c", [P, NT, 2])
        ve, rstd, neg_half = sb("ve_c", [P, NT]), sb("rstd_c", [P, NT]), sb("neg_half_c", [P, NT])
        lane = [NS(xt=sb(f"xt{i}", [P, D]), xT=sb(f"xT_{i}", [P, 2, P]), h=sb(f"h{i}", [P, FH]),
                   hT=[sb(f"h{l}T_{i}", [P, FH // P, P]) for l in (1, 2)], y=sb(f"y_{i}", [P, D]),
                   bt=ctx.enter_context(nc.psum_tensor(f"bt{i}", [P, 512], F32)),
                   bh=ctx.enter_context(nc.psum_tensor(f"bh{i}", [P, 512], F32)),
                   by=ctx.enter_context(nc.psum_tensor(f"by{i}", [P, 512], F32)),
                   pe=sem(f"lane{i}_pe"), dve=sem(f"lane{i}_dve"), act=sem(f"lane{i}_act"),
                   x_in=sem(f"lane{i}_x_in"), y_out=sem(f"lane{i}_y_out")) for i in range(2)]
        route = ctx.enter_context(nc.psum_tensor("route", [P, 512], F32))
        x_banks = [lane[0].bt, lane[0].bh, lane[1].bt, lane[1].bh]
        small, weights, made = sem("small_in"), [sem(f"w{e}_in") for e in range(NE)], sem("made_c")
        experts_in, bias_in, pe_r, chain = sem("experts_in"), sem("bias_in"), sem("pe_route"), sem("chain_c")
        exp_done, slots_ready, routed, scattered = sem("exp_done"), sem("slots_ready"), sem("routed"), sem("scattered")
        got = [sem(f"gathered{t}_in") for t in range(NT)]
        var_ready, rstd_ready, final, turnstile = sem("var_c"), sem("rstd_c_ready"), sem("final"), sem("turnstile_c")
        out_written = sem("out_written")
        hot_ready, away_ready = sem("hot_ready"), sem("away_ready")
        MADE = 5
        block = ctx.enter_context(nc.Block())

        HALVES = (slice(0, NT // 2), slice(NT // 2, NT))
        EARLY = 3

        def load_expert(eng, e):
            at = 0
            for name, k, n in (("W1", D // P, FH), ("W2", FH // P, FH), ("W3", FH // P, D)):
                eng.dma_start(w[:, e * WE + at:e * WE + at + k * n].rearrange("p (k n) -> p k n", k=k),
                              a[name][e, :, :].rearrange("(k p) n -> p k n", p=P)).then_inc(weights[e], 16)
                at += k * n

        @block.sync
        def _(sp):
            for dst, src in ((wg[:, :, :], a["wg"].rearrange("(k p) e -> p k e", p=P)), (bg[:, :], a["bg"].partition_broadcast(P))):
                sp.dma_start(dst, src).then_inc(small, 16)
            sp.dma_start(bias[:, :], bias_parts).then_inc(bias_in, 16)
            for e in range(EARLY):
                load_expert(sp, e)
            sp.wait_ge(scattered, 16 * 2 * NT)

            def load(l, s):
                sp.dma_start(l.xt[:, :], slots_x[bass.ds(s * P, P), :]).then_inc(l.x_in, 16)

            def store(l, s, i):
                sp.wait_ge(l.dve, 4 * i + (4 + 4))
                sp.sem_inc(turnstile, 1)
                sp.dma_start(slots_y[bass.ds(s * P, P), :], l.y[:, :]).then_inc(l.y_out, 16)

            for n, l in enumerate(lane):
                load(l, n)
            with sp.Fori(0, TILES // 2 - 1) as i:
                for n, l in enumerate(lane):
                    sp.wait_ge(l.pe, 6 * i + 1)
                    sp.sem_inc(turnstile, 1)
                    load(l, 2 * i + (2 + n))
                for n, l in enumerate(lane):
                    store(l, 2 * i + n, i)
            last = TILES // 2 - 1
            for n, l in enumerate(lane):
                store(l, 2 * last + n, last)
            for i, tiles in enumerate(HALVES):
                sp.wait_ge(final, i + 1)
                sp.dma_start(out.rearrange("b (q p) d -> p (b q) d", p=P)[:, tiles, :], gathered[:, tiles, 0, :])\
                    .then_inc(out_written, 16)
            sp.wait_ge(out_written, 32)

        @block.gpsimd
        def _(pool):
            G = nc.gpsimd
            count = Tally(made)

            def did(ins):
                ins.then_inc(made, 1)
                count.n += 1
                pool.wait_ge(made, count.value())

            def rstd_of(i):
                pool.wait_ge(var_ready, i + 1)
                G.tensor_tensor(rstd[:, HALVES[i]], ve[:, HALVES[i]], neg_half[:, HALVES[i]], ALU.pow).then_inc(rstd_ready, 1)

            did(G.memset(ones[:, :], 1.0))
            did(G.affine_select(out=tri[:, :], in_=ones[:, :], compare_op=ALU.is_gt, fill=0.0, base=0,
                                pattern=[[1, P]], channel_multiplier=-1))
            did(G.iota(counting[:, :], pattern=[[1, TILES]], base=0, channel_multiplier=0))
            did(G.memset(neg_half[:, :], -0.5))
            did(G.memset(ones_ne[:, :], 1.0))
            pool.wait_ge(slots_ready, 1)
            for t in range(NT):
                for c in range(2):
                    G.indirect_dma_start(out=slots_x[:, :], out_offset=bass.IndirectOffsetOnAxis(ap=slot[:, t, c:c + 1], axis=0),
                                         in_=x2[:, t, :], in_offset=None).then_inc(scattered, 16)
            for e in range(NE):
                if e >= EARLY:
                    load_expert(pool, e)
                pool.wait_ge(weights[e], 48)
                pool.sem_inc(experts_in, 1)
            for l in lane:
                pool.wait_ge(l.y_out, 16 * (TILES // 2 + 1))
            for t in range(NT):
                if t == NT - 2:
                    rstd_of(0)
                for c in range(2):
                    G.indirect_dma_start(out=gathered[:, t, c, :], out_offset=None, in_=slots_y[:, :],
                                         in_offset=bass.IndirectOffsetOnAxis(ap=slot[:, t, c:c + 1], axis=0)).then_inc(got[t], 16)
            rstd_of(1)

        @block.tensor
        def _(pe):
            for t in range(NT):
                for k in range(2):
                    last = nc.tensor.transpose(x_banks[t // 2][:, (2 * (t % 2) + k) * P:(2 * (t % 2) + k + 1) * P],
                                               x2[:, t, k * P:(k + 1) * P], ident[:, :])
                if t % 2:
                    last.then_inc(pe_r, 1)
            pe.wait_ge(chain, 4)
            pe.wait_ge(small, 32)
            pe.wait_ge(made, MADE)
            for t in range(NT):
                for k in range(2):
                    last = nc.tensor.matmul(route[:, t * NE:(t + 1) * NE], x2T[:, 2 * t + k, :], wg[:, k, :],
                                            start=(k == 0), stop=(k == 1))
            last.then_inc(pe_r, 1)
            pe.wait_ge(hot_ready, 1)
            for t in range(NT):
                for before in range(t + 1):
                    nc.tensor.matmul(route[:, 128 + t * NE:128 + (t + 1) * NE], tri[:, :] if before == t else ones[:, :],
                                     both[:, before, :], start=(before == 0), stop=(before == t))
            for t in range(NT):
                last = nc.tensor.matmul(route[:, 256:256 + NE], ones[:, :], both[:, t, :], start=(t == 0), stop=(t == NT - 1))
            last.then_inc(pe_r, 1)
            pe.wait_ge(routed, 1)
            pe.wait_ge(bias_in, 16)

            def transposes(l, src, n):
                for k in range(n):
                    last = nc.tensor.transpose(l.bt[:, k * P:(k + 1) * P], src[:, k * P:(k + 1) * P], ident[:, :])
                last.then_inc(l.pe, 1)

            def layer(l, bank, xT, k_tiles, n, e, at, bias_at):
                nc.tensor.matmul(bank[:, 0:n], ones[0:PARTS, :], bias[0:PARTS, bass.ds(e * BE + bias_at, n)], start=True, stop=False)
                for k in range(k_tiles):
                    last = nc.tensor.matmul(bank[:, 0:n], xT[:, k, :], w[:, bass.ds(e * WE + (at + k * n), n)],
                                            start=False, stop=(k == k_tiles - 1))
                last.then_inc(l.pe, 1)

            def x_transposes(l, i):
                pe.wait_ge(l.x_in, 16 * i + 16)
                pe.wait_ge(l.dve, 4 * i + 3)
                transposes(l, l.xt, 2)

            def pair(i, last):
                es = []
                for n, l in enumerate(lane):
                    es.append(pe.value_load(expert[0:1, bass.ds(2 * i + n, 1)], min_val=0, max_val=NE - 1))
                for l, e in zip(lane, es):
                    pe.wait_ge(l.dve, 4 * i + (4 + 1))
                    pe.wait_ge(l.act, 2 * i + 1)
                    pe.wait_ge(experts_in, e + 1)
                    layer(l, l.bh, l.xT, D // P, FH, e, 0, 0)
                for l in lane:
                    pe.wait_ge(l.act, 2 * i + 2)
                    transposes(l, l.h, 4)
                for l, e in zip(lane, es):
                    pe.wait_ge(l.dve, 4 * i + (4 + 2))
                    layer(l, l.bh, l.hT[0], FH // P, FH, e, 2 * FH, FH)
                for l in lane:
                    pe.wait_ge(l.act, 2 * i + 3)
                    transposes(l, l.h, 4)
                for l, e in zip(lane, es):
                    pe.wait_ge(l.dve, 4 * i + (4 + 3))
                    layer(l, l.by, l.hT[1], FH // P, D, e, 6 * FH, 2 * FH)
                    if not last:
                        x_transposes(l, i + 1)

            for l in lane:
                x_transposes(l, 0)
            with pe.Fori(0, TILES // 2 - 1) as i:
                pair(i, False)
            pair(TILES // 2 - 1, True)

        @block.scalar
        def _(act):
            for l in lane:
                act.sem_inc(l.act, 1)
            act.wait_ge(away_ready, 1)
            nc.scalar.activation(expd[:, :, :], away[:, :, :], ACT.Exp).then_inc(exp_done, 1)
            with act.Fori(0, TILES // 2) as i:
                for layer in range(2):
                    for l in lane:
                        act.wait_ge(l.pe, 6 * i + (2 + 2 * layer))
                        nc.scalar.activation(l.h[:, :], l.bh[:, :], ACT.Gelu).then_inc(l.act, 1)

        @block.vector
        def _(dve):
            V = nc.vector
            ch = Tally(chain)

            def link(ins):
                ins.then_inc(chain, 1)
                ch.n += 1
                dve.wait_ge(chain, ch.value())

            for l in lane:
                dve.sem_inc(l.dve, 4)
                dve.sem_inc(l.y_out, 16)
            for j in range(4):
                dve.wait_ge(pe_r, j + 1)
                V.tensor_copy(x2T[:, 4 * j:4 * j + 4, :].rearrange("p k q -> p (k q)"), x_banks[j][:, :]).then_inc(chain, 1)
                ch.n += 1
            dve.wait_ge(made, MADE)
            link(V.tensor_copy(count_f[:, :], counting[:, :]))
            link(V.tensor_scalar(count_128[:, :], count_f[:, 0:NE], float(P), None, ALU.mult))
            dve.wait_ge(small, 32)
            dve.wait_ge(pe_r, 5)
            link(V.tensor_tensor(logits[:, :, :], route[:, 0:NT * NE].rearrange("p (t e) -> p t e", t=NT),
                                 bg[:, :].unsqueeze(1).to_broadcast([P, NT, NE]), ALU.add))
            for t in range(NT):
                ins = V.max(best[:, t, :], logits[:, t, :])
            link(ins)
            for t in range(NT):
                ins = V.max_index(best_at[:, t, :], best[:, t, :], logits[:, t, :])
            link(ins)
            V.tensor_tensor(away[:, :, :], best[:, :, :], best[:, :, 0:1].to_broadcast([P, NT, NE]), ALU.subtract).then_inc(away_ready, 1)
            link(V.tensor_copy(best_f[:, :, :], best_at[:, :, 0:2]))
            link(V.tensor_tensor(hot[:, :, :, :], count_f[:, 0:NE].unsqueeze(1).unsqueeze(1).to_broadcast([P, NT, 2, NE]),
                                 best_f[:, :, :].unsqueeze(3).to_broadcast([P, NT, 2, NE]), ALU.is_equal))
            V.tensor_tensor(both[:, :, :], hot[:, :, 0, :], hot[:, :, 1, :], ALU.add).then_inc(hot_ready, 1)
            dve.wait_ge(pe_r, 6)
            link(V.tensor_tensor(many[:, :, :], route[:, 256:256 + NE].unsqueeze(2).to_broadcast([P, NE, NE]),
                                 count_128[:, :].unsqueeze(1).to_broadcast([P, NE, NE]), ALU.is_gt))
            link(V.tensor_reduce(tiles_of[:, :], many[:, :, :], X, ALU.add))
            link(V.tensor_tensor_scan(end[:, :], ones_ne[:, :], tiles_of[:, :], 0.0, ALU.mult, ALU.add))
            link(V.tensor_tensor(first[:, :], end[:, :], tiles_of[:, :], ALU.subtract))
            link(V.tensor_scalar(tiles_of[:, :], first[:, :], float(P), None, ALU.mult))
            link(V.tensor_tensor(place[:, :, :], route[:, 128:128 + NT * NE].rearrange("p (t e) -> p t e", t=NT),
                                 tiles_of[:, :].unsqueeze(1).to_broadcast([P, NT, NE]), ALU.add))
            link(V.tensor_tensor(place_hot[:, :, :, :], hot[:, :, :, :],
                                 place[:, :, :].unsqueeze(2).to_broadcast([P, NT, 2, NE]), ALU.mult))
            link(V.tensor_reduce(slot_f[:, :, :], place_hot[:, :, :, :], X, ALU.add))
            V.tensor_copy(slot[:, :, :], slot_f[:, :, :]).then_inc(slots_ready, 1)
            link(V.tensor_tensor(past[:, :, :], count_f[:, :].unsqueeze(2).to_broadcast([P, TILES, NE]),
                                 end[:, :].unsqueeze(1).to_broadcast([P, TILES, NE]), ALU.is_ge))
            link(V.tensor_reduce(expert_f[:, 0, :], past[:, :, :], X, ALU.add))
            link(V.tensor_scalar(expert_f[:, 1, :], expert_f[:, 0, :], float(NE - 1), None, ALU.min))
            V.tensor_copy(expert[:, :], expert_f[:, 1, :]).then_inc(routed, 1)
            dve.wait_ge(exp_done, 1)
            link(V.tensor_reduce(total[:, 0, :], expd[:, :, :], X, ALU.add))
            link(V.reciprocal(total[:, 1, :], total[:, 0, :]))
            link(V.tensor_tensor(gate[:, :, :], expd[:, :, 0:2], total[:, 1, :].unsqueeze(2).to_broadcast([P, NT, 2]), ALU.mult))
            def take_xT(l, i):
                dve.wait_ge(l.pe, 6 * i + 1)
                V.tensor_copy(l.xT[:, :, :].rearrange("p k q -> p (k q)"), l.bt[:, 0:D]).then_inc(l.dve, 1)

            def pair(i, last):
                for step in range(2):
                    for l in lane:
                        dve.wait_ge(l.pe, 6 * i + (3 + 2 * step))
                        V.tensor_copy(l.hT[step][:, :, :].rearrange("p k q -> p (k q)"), l.bt[:, :]).then_inc(l.dve, 1)
                for l in lane:
                    dve.wait_ge(l.pe, 6 * i + 6)
                    dve.wait_ge(l.y_out, 16 * i + 16)
                    V.tensor_copy(l.y[:, :], l.by[:, 0:D]).then_inc(l.dve, 1)
                    if not last:
                        take_xT(l, i + 1)

            for l in lane:
                take_xT(l, 0)
            with dve.Fori(0, TILES // 2 - 1) as i:
                pair(i, False)
            pair(TILES // 2 - 1, True)
            def normalise(half):
                dve.wait_ge(rstd_ready, half + 1)
                for t in range(NT)[HALVES[half]]:
                    ins = V.tensor_scalar(gathered[:, t, 0, :], y[:, t, :], mv[:, t, 0:1], rstd[:, t:t + 1],
                                          ALU.subtract, ALU.mult)
                ins.then_inc(final, 1)

            for i, tiles in enumerate(HALVES):
                for t in range(NT)[tiles]:
                    if t == NT - 2:
                        normalise(0)
                    dve.wait_ge(got[t], 32)
                    for c in range(2):
                        base = x2[:, t, :] if c == 0 else y[:, t, :]
                        link(V.scalar_tensor_tensor(out=y[:, t, :], in0=gathered[:, t, c, :], scalar=gate[:, t, c:c + 1],
                                                    in1=base, op0=ALU.mult, op1=ALU.add))
                    link(V.bn_stats(stats[:, t, :], y[:, t, :]))
                    dve.sem_inc(turnstile, 1)
                    link(V.bn_aggr(mv[:, t, :], stats[:, t, :]))
                V.tensor_scalar(ve[:, tiles], mv[:, tiles, 1], EPS, None, ALU.add).then_inc(var_ready, 1)
            normalise(1)



def program(nc, a, out):
    ca, cx = finish_shape(self_attention_shape()), finish_shape(cross_attention_shape())
    scratch = {c.name: nc.dram_tensor(f"parts_{c.name}", [2, PARTS, P, S + c.T], BF16, kind="Internal").ap()
               for c in (ca, cx)}
    outer = ExitStack()
    with outer:
        x2, ident, ident_bf = (outer.enter_context(nc.sbuf_tensor(n, sh, dt)) for n, sh, dt in (
            ("x_in_out", [P, NT, D], F32), ("ident", [P, P], F32), ("ident_bf", [P, P], BF16)))
        slots_x = nc.dram_tensor("slots_x", [TILES * P, D], F32, kind="Internal").ap()
        bias_parts = nc.dram_tensor("bias_parts", [PARTS, NE * BE], BF16, kind="Internal").ap()
        attention_block(nc, a, ca, cx, scratch, x2, ident, ident_bf, slots_x, bias_parts)
        experts_block(nc, a, out, x2, ident, slots_x, bias_parts)


def attention_block(nc, a, ca, cx, scratch, x2, ident, ident_bf, slots_x, bias_parts):
    ctx = ExitStack()
    with ctx:
        def sb(name, shape, dt=F32):
            return ctx.enter_context(nc.sbuf_tensor(name, shape, dt))

        def ps(name, w):
            return ctx.enter_context(nc.psum_tensor(name, [P, w], F32))

        mbank = [ps(f"m_bank{i}", 512) for i in range(M_RING)]
        stbank = [ps(f"st_bank{i}", 1024) for i in range(ST_RING)]
        obank = ps("o_bank", 512)

        loaded = ctx.enter_context(nc.semaphore("loaded"))
        made = ctx.enter_context(nc.semaphore("made"))
        loaded_cross, made_cross, made_stack0 = (ctx.enter_context(nc.semaphore(n))
                                                 for n in ("loaded_cross", "made_cross", "made_stack0"))
        sa, sx, ring = attention_sems(ctx, nc, ca), attention_sems(ctx, nc, cx), ring_sems(ctx, nc)

        x0 = x2
        x1 = sb("x1", [P, NT, D])
        common = dict(mbank=mbank, stbank=stbank, obank=obank, loaded=loaded, loaded_cross=loaded_cross, made=made, made_cross=made_cross, made_stack0=made_stack0, ident=ident, ident_bf=ident_bf)
        common.update(
            probs=[sb(f"probs{i}", [P, 1024]) for i in range(PROB_RING)],
            mparts=sb("max_parts", [P, 2 * UH, PARTS], BF16), nm=sb("neg_max", [P, 2, 2 * UH]),
            oT_unit=sb("oT_unit", [P, S]), rden=sb("rden", [P, 2, UH]), o_tm=sb("o_tokens", [P, 2, D]),
            oT=sb("oT", [P, 2, S]), y=sb("y", [P, 2, D]), y2=sb("y_biased", [P, 2, D]), stats=sb("stats", [P, 2, 6]),
            mv=sb("mean_var", [P, 2, 2]), ve=sb("var_and_mean", [P, 2, 2]), rstd=sb("rstd", [P, 2, 2]),
            neg_half=sb("neg_half", [P, 2]), qs=sb("quant_scale", [P, 3, 2]),
            qa=sb("quant_a", [P, 2, D]), qb=sb("quant_b", [P, 2, D]),
            cmask=sb("causal_mask", [P, 2, S]), junk=sb("masked_scores", [P, 2 * UH, S]),
            qst=[sb(f"q_stack{m}", [P, HH, S], BF16) for m in range(2)],
            )
        kst = [sb(f"k_stack{m}", [P, HH, SK], BF16) for m in range(2)]
        vaug = [sb(f"v_ones{m}", [P, len(cx.tiles), HH, VW]) for m in range(2)]
        f = sb("qk_rows", [P, S + SK])
        parts = sb("qk_parts", [P, PARTS, S + SK], BF16)
        parts_sa = sb("qk_parts_self", [P, PARTS, 2 * S], BF16)
        xT = sb("ctxT", [P, 2, SK])
        xTs = sb("xT", [P, 2, S])
        wts = {n: sb(n, [P, 2, D]) for n in ("w_q", "w_k", "w_v", "w_o", "xw_q", "xw_p", "xw_qq", "xw_pq",
                                             "xw_k", "xw_v")}
        bq, bk = sb("bq", [P, 2]), sb("bk", [P, 2])
        bv, bp = sb("bv", [P, D]), sb("bp", [P, D])

        ta = NS(**{**common, "mx": sb("row_max_self", [P, 2 * UH, 1]), "kst": kst, "vaug": vaug, "f": sb("qk_rest", [P, 2 * S]),
                   "parts": parts_sa, "xT": xTs, "wq": wts["w_q"], "wk": wts["w_k"],
                   "wv": wts["w_v"], "wo": wts["w_o"], "x_in": x0, "x_out": x1})
        tx = NS(**{**common, "mx": sb("row_max", [P, 2 * UH, cx.NC]), "kst": kst, "vaug": vaug, "f": f,
                   "parts": parts, "xT": xT, "wq": wts["xw_q"], "wk": wts["xw_k"], "wv": wts["xw_v"],
                   "wo": wts["xw_p"], "wq_raw": wts["xw_q"], "wp_raw": wts["xw_p"], "wq_q": wts["xw_qq"],
                   "wp_q": wts["xw_pq"], "xq": sb("x_quant", [P, 2, D]), "oq": sb("o_quant", [P, 2, D]),
                   "xqT": sb("xqT", [P, 2, S]), "bq": bq, "bk": bk, "bv": bv, "bp": bp, "x_in": x1, "x_out": x2})
        BW = NE * BE // P
        zeros, bias, bias_split = sb("zeros", [P, D]), sb("bias", [P, BW]), sb("bias_split", [P, PARTS, BW], BF16)
        experts_ready = ctx.enter_context(nc.semaphore("experts_ready"))
        rows = lambda w: w.rearrange("(k p) n -> p k n", p=P)
        loads = [(wts["w_q"], rows(a["w_q"])),
                 (wts["w_k"], rows(a["w_k"])), (wts["w_v"], rows(a["w_v"])), (wts["w_o"], rows(a["w_o"])),
                 (x0, a["x"].rearrange("b (q p) d -> p (b q) d", p=P)),
                 (wts["xw_q"], rows(a["xw_q"])), (wts["xw_p"], rows(a["xw_p"])),
                 (wts["xw_k"], rows(a["xw_kvT"][:, 0:D])), (wts["xw_v"], rows(a["xw_kvT"][:, D:2 * D])),
                 (bq, a["bq"]), (bk, a["bkv"][:, 0:2]), (bv, a["bv"].partition_broadcast(P)), (bp, a["bp"].partition_broadcast(P)),
                 (bias, a["bias"].rearrange("e (p f) -> (e p) f", f=BW))]
        SELF_LOADS = 3
        ta.made_all = MADE = 11
        ta.cross_loads = tx.cross_loads = 16 * (len(loads) - SELF_LOADS)
        la = NS(c=ca, s=sa, t=ta, x_dram=a["xT"], scratch=scratch["sa"])
        lx = NS(c=cx, s=sx, t=tx, x_dram=a["ctxT"], scratch=scratch["xa"])
        MADE_FIRST = 7
        block = ctx.enter_context(nc.Block())

        @block.scalar
        def _(act):
            for n, (dst, src) in enumerate(loads):
                act.dma_start(dst[:, :, :] if len(dst.shape) == 3 else dst[:, :], src)\
                    .then_inc(loaded if n < SELF_LOADS else loaded_cross, 16)
            act.dma_start(lx.t.xT[:, :, :], lx.x_dram[0, :, :].rearrange("(k p) t -> p k t", p=P)).then_inc(lx.s.x_loaded, 16)
            act_attention(nc, act, ring, la, lx)

        @block.gpsimd
        def _(pool):
            G = nc.gpsimd
            count, count_cross = Tally(made), Tally(made_cross)

            def did(ins, count=count):
                ins.then_inc(count.sem, 1)
                count.n += 1
                pool.wait_ge(count.sem, count.value())

            did(G.memset(ident[:, :], 0.0))
            did(G.memset(ident_bf[:, :], 0.0))
            did(G.memset(common["cmask"][:, :, :], 0.0))
            did(G.memset(common["neg_half"][:, :], -0.5))
            for w in (ident, ident_bf):
                did(G.affine_select(out=w[:, :], in_=w[:, :], compare_op=ALU.not_equal, fill=1.0, base=0,
                                pattern=[[-1, P]], channel_multiplier=1))
            did(G.affine_select(out=common["cmask"][:, :, :], in_=common["cmask"][:, :, :], compare_op=ALU.is_ge, fill=MASK,
                            base=0, pattern=[[P, 2], [-1, S]], channel_multiplier=1))
            assert count.n == MADE_FIRST
            for m in range(2):
                did(G.memset(kst[m][MROW:STACK, :, 0:S], 1.0))
                did(G.memset(vaug[m][:, :, :, DH:VW], 1.0))
            assert count.n == MADE

            def fill_rest():
                did(G.memset(kst[1][MROW:STACK, :, S:], 1.0), count_cross)
                did(G.memset(zeros[:, :], 0.0), count_cross)
                pool.wait_ge(loaded_cross, ta.cross_loads)
                for n in range(PARTS):
                    did(G.tensor_copy(bias_split[:, n, :], bias[:, :]), count_cross)
                    if n < PARTS - 1:
                        did(G.tensor_tensor(bias[:, :], bias[:, :], bias_split[:, n, :], ALU.subtract), count_cross)

            pool_attention(nc, pool, ring, la, lx, fill_rest)

        @block.vector
        def _(dve):
            dve.wait_ge(made, MADE_FIRST)
            dve.wait_ge(loaded, 16 * SELF_LOADS)
            dve_attention(nc, dve, ring, la, lx)

        @block.tensor
        def _(pe):
            pe.wait_ge(made, MADE_FIRST)
            pe.wait_ge(loaded, 16 * SELF_LOADS)
            nc.tensor.matmul(obank[:, 0:S], ident[:, :], common["cmask"][:, 0, :], start=True, stop=True)
            pe_attention(nc, pe, ring, la, lx)

        @block.sync
        def _(sp):
            def fill_for_experts():
                sp.wait_ge(made_cross, 7)
                sp.dma_start(slots_x.rearrange("(s p) d -> p s d", p=P),
                             zeros[:, :].unsqueeze(1).to_broadcast([P, TILES, D])).then_inc(experts_ready, 16)
                sp.dma_start(bias_parts.rearrange("s (p f) -> p s f", p=P), bias_split[:, :, :]).then_inc(experts_ready, 16)

            sp_attention(nc, sp, ring, la, lx, fill_for_experts)
            sp.wait_ge(experts_ready, 32)


def kernel(**inputs):
    import numpy as np
    import concourse.bacc as bacc
    from concourse import mybir as mb
    from concourse.bass_utils import run_bass_kernel_spmd

    g = {k: np.asarray(v) for k, v in inputs.items()}
    arrays = {
        "x": g["x"], "xT": g["x"].transpose(0, 2, 1), "ctxT": g["ctx_2048"].transpose(0, 2, 1),
        "w_q": g["L0_attn_q_wei"], "w_k": g["L0_attn_k_wei"], "w_v": g["L0_attn_v_wei"], "w_o": g["L0_attn_out_wei"],
        "xw_q": g["L0_xattn_wq"], "xw_p": g["L0_xattn_wp"], "xw_kvT": g["L0_xattn_wkv"].T,
        "bq": g["L0_xattn_bq"].reshape(2, 128).T, "bkv": g["L0_xattn_bkv"].reshape(4, 128).T,
        "W1": g["L0_ffn_W1"], "W2": g["L0_ffn_W2"], "W3": g["L0_ffn_W3"], "wg": g["L0_ffn_Wg"], "bg": g["L0_ffn_bg"],
        "bias": np.concatenate([g["L0_ffn_b1"], g["L0_ffn_b2"], g["L0_ffn_b3"]], axis=1),
        "bv": g["L0_xattn_bkv"][256:], "bp": g["L0_xattn_bp"],
    }
    arrays = {k: np.ascontiguousarray(v) for k, v in arrays.items()}
    nc = bacc.Bacc("TRN2", target_bir_lowering=False, num_devices=1)
    aps = {k: nc.dram_tensor("in_" + k, v.shape, mb.dt.from_np(v.dtype), kind="ExternalInput").ap() for k, v in arrays.items()}
    out = nc.dram_tensor("out_0", (4, 256, 256), mb.dt.float32, kind="ExternalOutput").ap()
    program(nc, aps, out)
    r = run_bass_kernel_spmd(nc, [{"in_" + k: v for k, v in arrays.items()}], core_ids=[0])
    return r.results[0]["out_0"]
```
